# Optimizing a Trainium2 kernel written in Bass

```python
import numpy as np
import jax
import jax.numpy as jnp

def _softmax(x, axis=-1):
    return jax.nn.softmax(x, axis=axis)
def _gelu(x):
    return jax.nn.gelu(x, approximate=True)
def _silu(x):
    return jax.nn.silu(x)
def _sigmoid(x):
    return jax.nn.sigmoid(x)
def _layernorm(x, axis=-1, eps=1e-5):
    m = jnp.mean(x, axis=axis, keepdims=True)
    v = jnp.var(x, axis=axis, keepdims=True)
    return (x - m) / jnp.sqrt(v + eps)
def _scatter_add(tgt, idx, src, axis=0):
    return tgt.at[idx].add(src)
def _segment_sum(src, seg, n):
    return jax.ops.segment_sum(src, seg, n)

kernel_name = 'mk_adj_preln_d2_adj_512_a17071'

def setup_inputs(seed: int = 0):
    np.random.seed(seed)
    _w = jnp.asarray
    def _rec_inputs():
        import jax
        import jax.numpy as jnp
        _gk = jax.random.key(seed)
        x = -0.0002928 + 1 * jax.random.normal(jax.random.fold_in(_gk, 1), (32, 512, 512), jnp.float32)
        _a = jax.random.bernoulli(jax.random.fold_in(_gk, 2), 0.015625, (512, 512))
        _a = jnp.logical_or(_a, jnp.eye(512, dtype=bool))
        _af = _a.astype(jnp.float32)
        adj = _af
        return x, adj
    x, adj = _rec_inputs()
    def _L0_gnn_setup():
        import jax, jax.numpy as jnp
        import numpy as np
        B, N, D = (4, 2048, 512)
        H, HD = (8, 64)
        key = jax.random.key(seed)
        ks = jax.random.split(key, 6)
        x = jax.random.normal(ks[0], (B, N, D), dtype=jnp.float32)
        adj = (jax.random.uniform(ks[1], (N, N)) < 0.1).astype(jnp.float32)
        adj = jnp.maximum(adj, jnp.eye(N, dtype=jnp.float32))
        s = 0.02
        Wq = jax.random.normal(ks[2], (D, H * HD), dtype=jnp.float32) * s
        Wk = jax.random.normal(ks[3], (D, H * HD), dtype=jnp.float32) * s
        Wv = jax.random.normal(ks[4], (D, H * HD), dtype=jnp.float32) * s
        bq = jnp.zeros((H * HD,), dtype=jnp.float32)
        bk = jnp.zeros((H * HD,), dtype=jnp.float32)
        bv = jnp.zeros((H * HD,), dtype=jnp.float32)
        return {'x': x, 'adj': adj, 'Wq': Wq, 'bq': bq, 'Wk': Wk, 'bk': bk, 'Wv': Wv, 'bv': bv}
    _L0_gnn_all = _L0_gnn_setup()
    _L0_gnn_in = {k: v for k, v in _L0_gnn_all.items() if k in ('Wq', 'bq', 'Wk', 'bk', 'Wv', 'bv', )}
    del _L0_gnn_all

    def _L1_gnn_setup():
        import jax, jax.numpy as jnp
        import numpy as np
        B, N, F_IN, F_OUT = (16, 2048, 512, 512)
        key = jax.random.key(seed)
        k1, k2, k3 = jax.random.split(key, 3)
        x = jax.random.normal(k1, (B, N, F_IN), dtype=jnp.float32)
        adj = jax.random.uniform(k2, (N, N), dtype=jnp.float32)
        bound = np.sqrt(6.0 / F_OUT)
        weight = jax.random.uniform(k3, (F_IN, F_OUT), dtype=jnp.float32, minval=-bound, maxval=bound)
        bias = jnp.zeros((F_OUT,), dtype=jnp.float32)
        return {'x': x, 'adj': adj, 'weight': weight, 'bias': bias}
    _L1_gnn_all = _L1_gnn_setup()
    _L1_gnn_in = {k: v for k, v in _L1_gnn_all.items() if k in ('weight', 'bias', )}
    del _L1_gnn_all

    return {
        "x": x,
        "adj": adj,
        "L0_gnn_Wq": _L0_gnn_in["Wq"],
        "L0_gnn_bq": _L0_gnn_in["bq"],
        "L0_gnn_Wk": _L0_gnn_in["Wk"],
        "L0_gnn_bk": _L0_gnn_in["bk"],
        "L0_gnn_Wv": _L0_gnn_in["Wv"],
        "L0_gnn_bv": _L0_gnn_in["bv"],
        "L1_gnn_weight": _L1_gnn_in["weight"],
        "L1_gnn_bias": _L1_gnn_in["bias"],
    }

def reference(x, adj, L0_gnn_Wq, L0_gnn_bq, L0_gnn_Wk, L0_gnn_bk, L0_gnn_Wv, L0_gnn_bv, L1_gnn_weight, L1_gnn_bias):
    import jax
    import jax.numpy as jnp
    def _L0_gnn_ref(x, adj, Wq, bq, Wk, bk, Wv, bv):
        import jax, jax.numpy as jnp
        import numpy as np
        B, N, D = (4, 2048, 512)
        H, HD = (8, 64)
        b, n, _ = x.shape
        q = (x @ Wq + bq).reshape(b, n, H, HD)
        k = (x @ Wk + bk).reshape(b, n, H, HD)
        v = (x @ Wv + bv).reshape(b, n, H, HD)
        scores = jnp.einsum('bihd,bjhd->bhij', q, k) / jnp.sqrt(jnp.float32(HD))
        mask = jnp.where(adj == 0, jnp.float32(-1000000000.0), jnp.float32(0.0))
        scores = scores + mask[None, None, :, :]
        weights = jax.nn.softmax(scores, axis=-1)
        out = jnp.einsum('bhij,bjhd->bihd', weights, v)
        return out.reshape(b, n, H * HD)

    def _L1_gnn_ref(x, adj, weight, bias):
        import jax, jax.numpy as jnp
        import numpy as np
        B, N, F_IN, F_OUT = (16, 2048, 512, 512)
        deg = adj.sum(axis=1)
        deg_inv_sqrt = jnp.where(deg > 0, jax.lax.rsqrt(deg), 0.0)
        norm_adj = adj * deg_inv_sqrt[:, None] * deg_inv_sqrt[None, :]
        support = jnp.einsum('bni,io->bno', x, weight)
        output = jnp.einsum('nm,bmo->bno', norm_adj, support)
        return output + bias

    h = jnp.maximum(_layernorm(x, axis=-1), 0.0)
    x = x + _L0_gnn_ref(h, adj, L0_gnn_Wq, L0_gnn_bq, L0_gnn_Wk, L0_gnn_bk, L0_gnn_Wv, L0_gnn_bv)
    h = jnp.maximum(_layernorm(x, axis=-1), 0.0)
    x = x + _L1_gnn_ref(h, adj, L1_gnn_weight, L1_gnn_bias)
    return x


_drawn_inputs = setup_inputs


def setup_inputs(seed=0):
    import zlib

    import numpy as np

    out = dict(_drawn_inputs(seed))
    spreads = {'L0_gnn_bq': (0.0, 0.8),
     'L0_gnn_bk': (0.0, 0.8),
     'L0_gnn_bv': (0.0, 0.1),
     'L1_gnn_bias': (0.0, 0.1)}
    factors = {'L0_gnn_Wq': 8.0, 'L0_gnn_Wk': 8.0}
    for name, (base, spread) in spreads.items():
        noise = np.random.default_rng([zlib.crc32(name.encode()), seed]).standard_normal(out[name].shape)
        drawn = base * np.exp(spread * noise) if base else spread * noise
        out[name] = jnp.asarray(drawn.astype(out[name].dtype))
    for name, factor in factors.items():
        out[name] = (out[name] * factor).astype(out[name].dtype)
    return out
```

```python
from contextlib import ExitStack

import concourse.bass as bass
from concourse import mybir

BATCH, TOK, DIM = 32, 512, 512
HEADS, HD = 8, 64
P = 128
TB = TOK // P
CB = DIM // P
PAIRS = HEADS // 2
GB = HEADS * TB
EPS = 1e-5
HI, LO = 0, 1
TERMS = ((HI, HI), (HI, LO), (LO, HI))
SCALE = HD ** -0.5
MASKED = 1e9

F32 = mybir.dt.float32
F32R = mybir.dt.float32r
ALU = mybir.AluOpType
ACT = mybir.ActivationFunctionType
AX_X = mybir.AxisListType.X

PLAN = (
    (("K", 1, 0), ("Q", 1, 0), ("V", 2, 0)),
    (("V", 3, 0), ("K", 2, 0)),
    (("Q", 2, 0), ("G", 0, -1)),
    (("K", 3, 0), ("Q", 3, 0), ("G", 1, -1)),
    (("G", 2, -1), ("G", 3, -1)),
    (("X", 0, 1), ("X", 1, 1), ("X", 2, 1), ("X", 3, 1), ("L", 0, -1), ("L", 1, -1)),
    (("K", 0, 1), ("Q", 0, 1), ("L", 2, -1)),
    (("L", 3, -1), ("V", 0, 1), ("V", 1, 1)),
)
BEFORE = tuple(("X", c, 0) for c in range(CB)) + tuple(("A", m, 0) for m in range(TB)) + (
    ("K", 0, 0), ("Q", 0, 0), ("V", 0, 0), ("V", 1, 0))
AFTER = tuple(("G", i, -1) for i in range(CB)) + tuple(("L", n, -1) for n in range(TB))


def groups(first, last):
    run = [("V", 0, 0), ("V", 1, 0)]
    out = []
    for step in PLAN:
        mine = []
        for g in step:
            if (first and g[2] < 0) or (last and g[2] > 0):
                continue
            mine.append((g, len(run) % 2, run[-2]))
            run.append(g)
        out.append(mine)
    return out


def straight(names, before):
    run = list(before)
    out = []
    for g in names:
        out.append((g, len(run) % 2, run[-2]))
        run.append(g)
    return out


def gnn_layers(nc, x, adj, wq, bq, wk, bk, wv, bv, w1, b1, out):
    with ExitStack() as ctx:
        def sb(name, shape, dt=F32):
            return ctx.enter_context(nc.sbuf_tensor(name, shape, dt))

        def bank(name):
            return ctx.enter_context(nc.psum_tensor(name, [P, 512], F32))

        def sem(name):
            return ctx.enter_context(nc.semaphore(name))

        WK = sb("WK", [P, 2, CB, DIM], F32R)
        WQ = sb("WQ", [P, 2, CB, DIM], F32R)
        WV = sb("WV", [P, 2, CB, DIM], F32R)
        W1 = sb("W1", [P, 2, CB, DIM], F32R)
        AT = sb("AT", [P, 2, TB, TOK], F32R)
        mask = sb("mask", [P, TB, TOK])
        bv_rows = sb("bv_rows", [P, DIM])
        b1_rows = sb("b1_rows", [P, DIM])
        bk_cols = sb("bk_cols", [P, PAIRS])
        bq_cols = sb("bq_cols", [P, PAIRS])
        ident = sb("ident", [P, P])
        hn = sb("hn", [P, TB, DIM])
        hT = sb("hT", [P, 2, CB, TOK], F32R)
        QS = sb("QS", [P, 2, 2, TOK], F32R)
        KS = sb("KS", [P, 2, 2, 2, TOK], F32R)
        VS = sb("VS", [P, TB, HEADS, 2, HD], F32R)
        probs = sb("probs", [P, 2, TB, TOK])
        PT = sb("PT", [P, 2, 2, TOK], F32R)
        osum = sb("osum", [P, TOK])
        att = sb("att", [P, TB, P])
        acc = sb("acc", [P, TB, DIM])
        res = sb("res", [P, TB, DIM])
        H1 = sb("H1", [P, 2, CB, TB, P], F32R)
        nmin = sb("nmin", [P, HEADS, TB])
        sums = sb("sums", [P, HEADS, TB])
        rsums = sb("rsums", [P, HEADS, TB])
        half = sb("half", [P, TB])
        deg = sb("deg", [P, TB])
        dpos = sb("dpos", [P, TB])
        dis = sb("dis", [P, TB])
        ln = [dict(stats=sb(f"stats{n}", [P, TB, 6]), mv=sb(f"mv{n}", [P, TB, 2]),
                   var=sb(f"var{n}", [P, TB]), rstd=sb(f"rstd{n}", [P, TB])) for n in range(2)]

        score_bank = [bank(f"score_bank{i}") for i in range(2)]
        turn_bank = [bank(f"turn_bank{i}") for i in range(2)]
        group_bank = [bank(f"group_bank{i}") for i in range(2)]
        o_bank = bank("o_bank")
        oturn_bank = bank("oturn_bank")

        x_loaded, acc_loaded = sem("x_loaded"), sem("acc_loaded")
        adj_loaded, cols_loaded, rows_loaded = sem("adj_loaded"), sem("cols_loaded"), sem("rows_loaded")
        wk_loaded, wq_loaded, wv_loaded, w1_loaded = (sem(f"w{n}_loaded") for n in "kqv1")
        k_doubled = sem("k_doubled")
        res_free = sem("res_free")
        consts_ready, ident_ready, w_hi, w_split = sem("consts_ready"), sem("ident_ready"), sem("w_hi"), sem("w_split")
        w_scaled, bq_scaled = sem("w_scaled"), sem("bq_scaled")
        deg_step, deg_pow, dis_ready, adj_scaled, mask_ready = (
            sem(n) for n in ("deg_step", "deg_pow", "dis_ready", "adj_scaled", "mask_ready"))
        psum_ready = {k: sem(f"{k}_psum") for k in "XAKQVGL"}
        hi_ready = {k: sem(f"{k}_hi") for k in "XAKQVG"}
        done = {k: sem(f"{k}_done") for k in "XAKQVGL"}
        dve_gate = sem("dve_gate")
        stats_done = [sem(f"stats_done{n}") for n in range(2)]
        moments_done = [sem(f"moments_done{n}") for n in range(2)]
        var_done = [sem(f"var_done{n}") for n in range(2)]
        rstd_done = [sem(f"rstd_done{n}") for n in range(2)]
        normed = [sem(f"normed{n}") for n in range(2)]
        h1_hi, h1_done = sem("h1_hi"), sem("h1_done")
        scores_ready, masked, exp_done = sem("scores_ready"), sem("masked"), sem("exp_done")
        turned, pt_hi, pt_done, pv_done = sem("turned"), sem("pt_hi"), sem("pt_done"), sem("pv_done")
        o_lower, o_done = sem("o_lower"), sem("o_done")
        o_turned, rsums_done, att_done, att_added = sem("o_turned"), sem("rsums_done"), sem("att_done"), sem("att_added")
        acc_biased, res_ready = sem("acc_biased"), sem("res_ready")

        def need(eng, s, count):
            if not isinstance(count, int) or count > 0:
                eng.wait_ge(s, count)

        def nth(group, b):
            kind, i, db = group
            return 4 * (b + db) + i + 1

        x_rows = x.rearrange("b (t p) d -> b p t d", p=P)
        out_rows = out.rearrange("b (t p) d -> b p t d", p=P)

        block = ctx.enter_context(nc.Block())

        @block.sync
        def _(sp):
            sp.dma_start(hn[:], x_rows[0]).then_inc(x_loaded, 16)
            sp.dma_start(probs[:, 0], wk.rearrange("(c p) n -> p c n", p=P)).then_inc(wk_loaded, 16)
            sp.dma_start(probs[:, 1], wq.rearrange("(c p) n -> p c n", p=P)).then_inc(wq_loaded, 16)
            sp.dma_start(bk_cols[:], bk.rearrange("(c p) -> p c", p=P), allow_slow_non_contiguous=True).then_inc(cols_loaded, 16)
            sp.dma_start(bq_cols[:], bq.rearrange("(c p) -> p c", p=P), allow_slow_non_contiguous=True).then_inc(cols_loaded, 16)
            sp.dma_start(mask[:], adj.rearrange("(t p) n -> p t n", p=P)).then_inc(adj_loaded, 16)
            sp.dma_start(acc[:], wv.rearrange("(c p) n -> p c n", p=P)).then_inc(wv_loaded, 16)
            sp.dma_start(res[:], w1.rearrange("(c p) n -> p c n", p=P)).then_inc(w1_loaded, 16)
            sp.dma_start(bv_rows[:], bv.partition_broadcast(P)).then_inc(rows_loaded, 16)
            sp.dma_start(b1_rows[:], b1.partition_broadcast(P)).then_inc(res_free, 16)

            def double_k(b, p):
                sp.wait_ge(done["K"], 4 * b + p + 1)
                sp.dma_start(KS[HD:P, p % 2, 0].bitcast(F32), KS[0:HD, p % 2, 0].bitcast(F32)).then_inc(k_doubled, 16)
                sp.dma_start(KS[0:HD, p % 2, 1].bitcast(F32), KS[HD:P, p % 2, 1].bitcast(F32)).then_inc(k_doubled, 16)

            def load_acc(b):
                need(sp, h1_done, TB * b)
                sp.dma_start(acc[:], x_rows[b]).then_inc(acc_loaded, 16)

            def store(b):
                for n in range(TB):
                    sp.wait_ge(done["L"], 4 * b + n + 1)
                    sp.dma_start(out_rows[b, :, n], res[:, n]).then_inc(res_free, 16)

            def batch(b, first=False, last=False):
                if not last:
                    sp.wait_ge(psum_ready["X"], CB * (b + 1))
                    sp.dma_start(hn[:], x_rows[b + 1]).then_inc(x_loaded, 16)
                double_k(b, 1)
                double_k(b, 2)
                if not first:
                    load_acc(b)
                double_k(b, 3)
                if not last:
                    double_k(b + 1, 0)
                if not first:
                    store(b - 1)

            sp.wait_ge(w_split, 3)
            load_acc(0)
            double_k(0, 0)
            batch(0, first=True)
            with sp.Fori(1, BATCH - 1) as b:
                batch(b)
            batch(BATCH - 1, last=True)
            store(BATCH - 1)
            sp.wait_ge(res_free, 16 + 16 * TB * BATCH)

        @block.tensor
        def _(pe):
            def product(psum, wide, moving, c, stop, cols=slice(0, 512)):
                for n, (l, r) in enumerate(TERMS):
                    mm = nc.tensor.matmul(psum[:, cols], wide(l), moving(r),
                                          start=(c == 0 and n == 0), stop=(stop and n == 2))
                return mm

            def piece(group, bank, before, b, c):
                kind, i, db = group
                psum = group_bank[bank]
                if c == 0:
                    if before is not None:
                        pe.wait_ge(done[before[0]], nth(before, b))
                    if kind in "KQV":
                        pe.wait_ge(done["X"], CB * (b + db + 1))
                    elif kind == "X":
                        pe.wait_ge(normed[0], TB * (b + db + 1))
                    elif kind == "A":
                        pe.wait_ge(adj_scaled, 1)
                    elif kind == "G":
                        pe.wait_ge(h1_done, TB * (b + db + 1))
                    elif kind == "L":
                        pe.wait_ge(done["G"], CB * (b + db + 1))
                last = c == 3
                if kind in "KQ":
                    w = WK if kind == "K" else WQ
                    mm = product(psum, lambda s: w[:, s, c, P * i:P * i + P], lambda s: hT[:, s, c], c, last)
                elif kind == "V":
                    j = 2 * (i % 2) + c // 2
                    cols = slice(256 * (c // 2), 256 * (c // 2) + 256)
                    for k in (2 * (c % 2), 2 * (c % 2) + 1):
                        mm = product(psum, lambda s: hT[:, s, k, P * j:P * j + P],
                                     lambda s: WV[:, s, k, 256 * (i // 2):256 * (i // 2) + 256], k, k == CB - 1, cols)
                elif kind == "G":
                    mm = product(psum, lambda s: H1[:, s, i, c], lambda s: AT[:, s, c], c, last)
                elif kind == "L":
                    mm = product(psum, lambda s: H1[:, s, c, i], lambda s: W1[:, s, c], c, last)
                else:
                    src = hn if kind == "X" else res
                    mm = nc.tensor.transpose(psum[:, P * c:P * c + P], src[:, c, P * i:P * i + P], ident[:])
                if last:
                    mm.then_inc(psum_ready[kind], 1)

            def scores(b, h, i):
                g, pair = GB * b + TB * h + i, h // 2
                if i == 0 and h % 2 == 0:
                    pe.wait_ge(done["Q"], PAIRS * b + pair + 1)
                    pe.wait_ge(k_doubled, 32 * (PAIRS * b + pair + 1))
                need(pe, exp_done, g - 1)
                for s in (HI, LO):
                    mm = nc.tensor.matmul(score_bank[i % 2][:], QS[:, pair % 2, h % 2, P * i:P * i + P],
                                          KS[:, pair % 2, h % 2, s], start=(s == HI), stop=(s == LO))
                mm.then_inc(scores_ready, 1)

            def turn(b, h, j):
                k = GB * b + TB * h + j
                if j == 0:
                    pe.wait_ge(exp_done, GB * b + TB * (h + 1))
                need(pe, pt_done, k - 1)
                for i in range(TB):
                    mm = nc.tensor.transpose(turn_bank[j % 2][:, P * i:P * i + P],
                                             probs[:, h % 2, i, P * j:P * j + P], ident[:])
                mm.then_inc(turned, 1)

            def weigh(b, h, j):
                k = GB * b + TB * h + j
                if j == 0:
                    need(pe, o_done, HEADS * b + h)
                    if h % 4 == 0:
                        pe.wait_ge(done["V"], 4 * b + 2 * (h // 4) + 2)
                pe.wait_ge(pt_done, k + 1)
                for s in (HI, LO):
                    mm = nc.tensor.matmul(o_bank[:], VS[:, j, h].rearrange("p s d -> p (s d)"), PT[:, j % 2, s],
                                          start=(j == 0 and s == HI), stop=(j == TB - 1 and s == LO))
                mm.then_inc(pv_done, 1)

            def turn_out(b, p):
                pe.wait_ge(o_done, HEADS * b + 2 * p + 2)
                need(pe, att_done, PAIRS * b + p)
                for i in range(TB):
                    mm = nc.tensor.transpose(oturn_bank[:, P * i:P * i + P], osum[:, P * i:P * i + P], ident[:])
                mm.then_inc(o_turned, 1)

            def batch(b, first=False, last=False):
                steps = groups(first, last)
                for h in range(HEADS):
                    mine = steps[h]
                    for q in range(TB):
                        if h + 1 < HEADS:
                            scores(b, h + 1, q)
                        elif not last:
                            scores(b + 1, 0, q)
                        for n in range(q * len(mine), (q + 1) * len(mine)):
                            piece(*mine[n // 4], b, n % 4)
                        turn(b, h, q)
                        if q > 0:
                            weigh(b, h, q - 1)
                        elif h > 0:
                            weigh(b, h - 1, TB - 1)
                        elif not first:
                            weigh(b - 1, HEADS - 1, TB - 1)
                        if q == 2 and h % 2 == 0:
                            if h > 0:
                                turn_out(b, h // 2 - 1)
                            elif not first:
                                turn_out(b - 1, PAIRS - 1)

            pe.wait_ge(ident_ready, 1)
            for n, (group, bank, before) in enumerate(straight(BEFORE, (None, None))):
                if group[0] in "KQV" and group[1] == 0:
                    pe.wait_ge(w_split, {"K": 1, "Q": 2, "V": 3}[group[0]])
                for c in range(4):
                    piece(group, bank, before, 0, c)
            for q in range(TB):
                scores(0, 0, q)
            pe.wait_ge(w_split, 4)
            pe.wait_ge(done["A"], TB)
            batch(0, first=True)
            with pe.Fori(1, BATCH - 1) as b:
                batch(b)
            batch(BATCH - 1, last=True)
            weigh(BATCH - 1, HEADS - 1, TB - 1)
            turn_out(BATCH - 1, PAIRS - 1)
            for group, bank, before in straight(AFTER, (("L", 2, -2), ("L", 3, -2))):
                for c in range(4):
                    piece(group, bank, before, BATCH, c)

        @block.scalar
        def _(act):
            def split_hi(w, raw, s, count):
                act.wait_ge(s, count)
                nc.scalar.copy(w[:, HI], raw).then_inc(w_hi, 1)

            def group_hi(group, bank, b):
                kind, i, db = group
                psum = group_bank[bank]
                if kind == "L":
                    return
                act.wait_ge(psum_ready[kind], nth(group, b))
                if kind in "KQ":
                    need(act, scores_ready, 2 * TB * (PAIRS * (b + db) + i - 1))
                    for e in range(2):
                        rows = slice(HD * e, HD * e + HD)
                        to = KS[rows, i % 2, e, HI] if kind == "K" else QS[rows, i % 2, e]
                        cols = bk_cols if kind == "K" else bq_cols
                        last = nc.scalar.activation(to, psum[rows, :], ACT.Identity, bias=cols[rows, i:i + 1])
                elif kind == "V":
                    need(act, pv_done, GB * (b + db - 1) + GB // 2 * (i // 2 + 1))
                    j, h = 2 * (i % 2), HEADS // 2 * (i // 2)
                    last = nc.scalar.copy(VS[:, j:j + 2, h:h + 4, HI],
                                          psum[:].rearrange("p (j h d) -> p j h d", j=2, d=HD))
                elif kind == "X":
                    last = nc.scalar.activation(hT[:, HI, i], psum[:], ACT.Relu)
                elif kind == "G":
                    last = nc.scalar.copy(H1[:, HI, i].rearrange("p t n -> p (t n)"), psum[:])
                elif kind == "A":
                    last = nc.scalar.mul(AT[:, HI, i], psum[:], dis[:, i:i + 1])
                last.then_inc(hi_ready[kind], 1)

            def exponent(b, h, i):
                g = GB * b + TB * h + i
                act.wait_ge(masked, g + 1)
                if i == 0:
                    need(act, turned, TB * (HEADS * b + h - 1))
                nc.scalar.activation(probs[:, h % 2, i], score_bank[i % 2][:], ACT.Exp, scale=-1.0,
                                     bias=nmin[:, h, i:i + 1], accum_out=sums[:, h, i:i + 1]).then_inc(exp_done, 1)

            def pt_hi_part(b, h, j):
                k = GB * b + TB * h + j
                act.wait_ge(turned, k + 1)
                need(act, pv_done, k - 1)
                nc.scalar.copy(PT[:, j % 2, HI], turn_bank[j % 2][:]).then_inc(pt_hi, 1)

            def o_lower_half(b, h):
                act.wait_ge(pv_done, GB * b + TB * (h + 1))
                need(act, o_turned, PAIRS * b + h // 2)
                rows = slice(HD * (h % 2), HD * (h % 2) + HD)
                nc.scalar.copy(osum[rows, :], o_bank[HD:P, :]).then_inc(o_lower, 1)

            def h1_hi_part(b, t):
                act.wait_ge(normed[1], TB * b + t + 1)
                nc.scalar.activation(H1[:, HI, :, t], acc[:, t].rearrange("p (c n) -> p c n", n=P),
                                     ACT.Relu).then_inc(h1_hi, 1)

            def batch(b, first=False, last=False):
                steps = groups(first, last)
                for h in range(HEADS):
                    mine = steps[h]
                    for q in range(TB):
                        if q == 1:
                            if h > 0:
                                o_lower_half(b, h - 1)
                            elif not first:
                                o_lower_half(b - 1, HEADS - 1)
                        if h + 1 < HEADS:
                            exponent(b, h + 1, q)
                        elif not last:
                            exponent(b + 1, 0, q)
                        for n in range(q * len(mine), (q + 1) * len(mine)):
                            if n % 4 == 3:
                                group_hi(mine[n // 4][0], mine[n // 4][1], b)
                        pt_hi_part(b, h, q)
                        if not first and (h, q) == (1, 3):
                            h1_hi_part(b - 1, 0)
                            h1_hi_part(b - 1, 1)
                        if not first and (h, q) == (2, 0):
                            h1_hi_part(b - 1, 2)
                            h1_hi_part(b - 1, 3)

            split_hi(WK, probs[:, 0], wk_loaded, 16)
            split_hi(WQ, probs[:, 1], w_scaled, 1)
            split_hi(WV, acc[:], wv_loaded, 16)
            split_hi(W1, res[:], w1_loaded, 16)
            act.wait_ge(bq_scaled, 1)
            act.wait_ge(cols_loaded, 32)
            act.wait_ge(dis_ready, 1)
            for group, bank, _ in straight(BEFORE, (None, None)):
                group_hi(group, bank, 0)
            act.wait_ge(w_split, 2)
            for q in range(TB):
                exponent(0, 0, q)
            batch(0, first=True)
            with act.Fori(1, BATCH - 1) as b:
                batch(b)
            batch(BATCH - 1, last=True)
            o_lower_half(BATCH - 1, HEADS - 1)
            for t in range(TB):
                h1_hi_part(BATCH - 1, t)
            for group, bank, _ in straight(AFTER, (("L", 2, -2), ("L", 3, -2))):
                group_hi(group, bank, BATCH)

        @block.vector
        def _(dve):
            def split_lo(w, raw, count):
                dve.wait_ge(w_hi, count)
                nc.vector.tensor_tensor(w[:, LO], raw, w[:, HI].bitcast(F32), ALU.subtract).then_inc(w_split, 1)

            def group_lo(group, bank, b):
                kind, i, db = group
                psum = group_bank[bank]
                if kind == "L":
                    dve.wait_ge(psum_ready["L"], nth(group, b))
                    last = nc.vector.tensor_tensor(res[:, i], psum[:], res[:, i], ALU.add)
                else:
                    dve.wait_ge(hi_ready[kind], nth(group, b))
                if kind in "KQ":
                    for e in range(2):
                        rows, other = slice(HD * e, HD * e + HD), slice(HD * (1 - e), HD * (1 - e) + HD)
                        hi = KS[rows, i % 2, e, HI] if kind == "K" else QS[rows, i % 2, e]
                        lo = KS[rows, i % 2, e, LO] if kind == "K" else QS[other, i % 2, e]
                        cols = bk_cols if kind == "K" else bq_cols
                        last = nc.vector.scalar_tensor_tensor(lo, psum[rows, :], cols[rows, i:i + 1],
                                                              hi.bitcast(F32), ALU.add, ALU.subtract)
                elif kind == "V":
                    j, h = 2 * (i % 2), HEADS // 2 * (i // 2)
                    last = nc.vector.tensor_tensor(VS[:, j:j + 2, h:h + 4, LO],
                                                   psum[:].rearrange("p (j h d) -> p j h d", j=2, d=HD),
                                                   VS[:, j:j + 2, h:h + 4, HI].bitcast(F32), ALU.subtract)
                elif kind == "X":
                    last = nc.vector.scalar_tensor_tensor(hT[:, LO, i], psum[:], 0.0, hT[:, HI, i].bitcast(F32),
                                                          ALU.max, ALU.subtract)
                elif kind == "G":
                    last = nc.vector.tensor_tensor(H1[:, LO, i].rearrange("p t n -> p (t n)"), psum[:],
                                                   H1[:, HI, i].rearrange("p t n -> p (t n)").bitcast(F32),
                                                   ALU.subtract)
                elif kind == "A":
                    last = nc.vector.scalar_tensor_tensor(AT[:, LO, i], psum[:], dis[:, i:i + 1],
                                                          AT[:, HI, i].bitcast(F32), ALU.mult, ALU.subtract)
                last.then_inc(done[kind], 1)

            def mask_scores(b, h, i):
                dve.wait_ge(scores_ready, GB * b + TB * h + i + 1)
                nc.vector.sem_inc(dve_gate, 1)
                nc.vector.tensor_tensor_reduce(score_bank[i % 2][:], score_bank[i % 2][:], mask[:, i], 1.0, 3.4e38,
                                               ALU.add, ALU.min, nmin[:, h, i:i + 1]).then_inc(masked, 1)

            def pt_lo_part(b, h, j):
                dve.wait_ge(pt_hi, GB * b + TB * h + j + 1)
                nc.vector.tensor_tensor(PT[:, j % 2, LO], turn_bank[j % 2][:], PT[:, j % 2, HI].bitcast(F32),
                                        ALU.subtract).then_inc(pt_done, 1)

            def o_add(b, h):
                dve.wait_ge(o_lower, HEADS * b + h + 1)
                rows = slice(HD * (h % 2), HD * (h % 2) + HD)
                nc.vector.tensor_tensor(osum[rows, :], o_bank[0:HD, :], osum[rows, :], ALU.add).then_inc(o_done, 1)

            def invert_sums(b, p):
                dve.wait_ge(exp_done, 2 * TB * (PAIRS * b + p + 1))
                nc.vector.reciprocal(rsums[:, 2 * p:2 * p + 2], sums[:, 2 * p:2 * p + 2]).then_inc(rsums_done, 1)

            def normalise_out(b, p):
                dve.wait_ge(rsums_done, PAIRS * b + p + 1)
                dve.wait_ge(o_turned, PAIRS * b + p + 1)
                need(dve, att_added, PAIRS * b + p)
                nc.vector.tensor_tensor(
                    att[:].rearrange("p i (h d) -> p i h d", d=HD),
                    oturn_bank[:].rearrange("p (i h d) -> p i h d", i=TB, d=HD),
                    rsums[:, 2 * p:2 * p + 2].rearrange("p h i -> p i h").unsqueeze(3).to_broadcast([P, TB, 2, HD]),
                    ALU.mult).then_inc(att_done, 1)

            def ln_stats(n, b, src, t):
                nc.vector.bn_stats(ln[n]["stats"][:, t], src[:, t]).then_inc(stats_done[n], 1)

            def ln_moments(n, b):
                for t in range(TB):
                    if t == 0:
                        dve.wait_ge(stats_done[n], TB * (b + 1))
                        nc.vector.sem_inc(dve_gate, 1)
                    nc.vector.bn_aggr(ln[n]["mv"][:, t], ln[n]["stats"][:, t]).then_inc(moments_done[n], 1)
                dve.wait_ge(moments_done[n], TB * (b + 1))
                nc.vector.tensor_scalar(ln[n]["var"][:], ln[n]["mv"][:, :, 1], EPS, None, ALU.add).then_inc(var_done[n], 1)

            def ln_apply(n, b, src):
                dve.wait_ge(rstd_done[n], b + 1)
                for t in range(TB):
                    nc.vector.tensor_scalar(src[:, t], src[:, t], ln[n]["mv"][:, t, 0:1], ln[n]["rstd"][:, t:t + 1],
                                            ALU.subtract, ALU.mult).then_inc(normed[n], 1)

            def h1_lo_part(b, t):
                dve.wait_ge(h1_hi, TB * b + t + 1)
                nc.vector.scalar_tensor_tensor(H1[:, LO, :, t], acc[:, t].rearrange("p (c n) -> p c n", n=P), 0.0,
                                               H1[:, HI, :, t].bitcast(F32), ALU.max, ALU.subtract).then_inc(h1_done, 1)

            def batch(b, first=False, last=False):
                steps = groups(first, last)
                for h in range(HEADS):
                    mine = steps[h]
                    for q in range(TB):
                        if h + 1 < HEADS:
                            mask_scores(b, h + 1, q)
                        elif not last:
                            mask_scores(b + 1, 0, q)
                        if q == 1:
                            if h > 0:
                                o_add(b, h - 1)
                            elif not first:
                                o_add(b - 1, HEADS - 1)
                        for n in range(q * len(mine), (q + 1) * len(mine)):
                            if n % 4 == 3:
                                group_lo(mine[n // 4][0], mine[n // 4][1], b)
                        pt_lo_part(b, h, q)
                        if h % 2 == 0 and (h > 0 or not first):
                            bb, p = (b, h // 2 - 1) if h > 0 else (b - 1, PAIRS - 1)
                            if q == 2:
                                invert_sums(bb, p)
                            if q == 3:
                                normalise_out(bb, p)
                        if not first:
                            if (h, q) == (1, 0):
                                dve.wait_ge(att_added, PAIRS * b)
                                ln_stats(1, b - 1, acc, 0)
                                ln_stats(1, b - 1, acc, 1)
                            if (h, q) == (1, 1):
                                ln_stats(1, b - 1, acc, 2)
                                ln_stats(1, b - 1, acc, 3)
                                ln_moments(1, b - 1)
                            if (h, q) == (1, 2):
                                dve.wait_ge(res_ready, b)
                                ln_apply(1, b - 1, acc)
                            if (h, q) == (1, 3):
                                h1_lo_part(b - 1, 0)
                                h1_lo_part(b - 1, 1)
                            if (h, q) == (2, 0):
                                h1_lo_part(b - 1, 2)
                                h1_lo_part(b - 1, 3)
                        if not last:
                            if (h, q) == (3, 0):
                                dve.wait_ge(x_loaded, 16 * (b + 2))
                                ln_stats(0, b + 1, hn, 0)
                                ln_stats(0, b + 1, hn, 1)
                            if (h, q) == (3, 1):
                                ln_stats(0, b + 1, hn, 2)
                                ln_stats(0, b + 1, hn, 3)
                            if (h, q) == (3, 2):
                                ln_moments(0, b + 1)
                            if (h, q) == (4, 0):
                                ln_apply(0, b + 1, hn)

            nc.vector.memset(half[:], -0.5).then_inc(consts_ready, 1)
            dve.wait_ge(x_loaded, 16)
            for t in range(TB):
                ln_stats(0, 0, hn, t)
            ln_moments(0, 0)
            dve.wait_ge(wq_loaded, 16)
            nc.vector.tensor_scalar(probs[:, 1], probs[:, 1], -SCALE, None, ALU.mult).then_inc(w_scaled, 1)
            dve.wait_ge(cols_loaded, 32)
            nc.vector.tensor_scalar(bq_cols[:], bq_cols[:], -SCALE, None, ALU.mult).then_inc(bq_scaled, 1)
            dve.wait_ge(adj_loaded, 16)
            nc.vector.tensor_reduce(deg[:], mask[:], AX_X, ALU.add).then_inc(deg_step, 1)
            dve.wait_ge(deg_step, 1)
            nc.vector.tensor_scalar(dpos[:], deg[:], 0.0, None, ALU.is_gt).then_inc(deg_step, 1)
            dve.wait_ge(deg_step, 2)
            nc.vector.tensor_scalar(deg[:], deg[:], 1.1754944e-38, None, ALU.max).then_inc(deg_step, 1)
            ln_apply(0, 0, hn)
            split_lo(WK, probs[:, 0], 1)
            split_lo(WQ, probs[:, 1], 2)
            split_lo(WV, acc[:], 3)
            split_lo(W1, res[:], 4)
            dve.wait_ge(deg_pow, 1)
            nc.vector.tensor_tensor(dis[:], dis[:], dpos[:], ALU.mult).then_inc(dis_ready, 1)
            dve.wait_ge(dis_ready, 1)
            dve.wait_ge(w_split, 4)
            for t in range(TB):
                last = nc.vector.tensor_scalar(res[:, t], mask[:, t], dis[:, t:t + 1], None, ALU.mult)
            last.then_inc(adj_scaled, 1)
            dve.wait_ge(adj_scaled, 1)
            nc.vector.tensor_scalar(mask[:], mask[:], 0.0, MASKED, ALU.is_equal, ALU.mult).then_inc(mask_ready, 1)
            for group, bank, _ in straight(BEFORE, (None, None)):
                group_lo(group, bank, 0)
            dve.wait_ge(mask_ready, 1)
            for q in range(TB):
                mask_scores(0, 0, q)
            batch(0, first=True)
            with dve.Fori(1, BATCH - 1) as b:
                batch(b)
            batch(BATCH - 1, last=True)
            o_add(BATCH - 1, HEADS - 1)
            invert_sums(BATCH - 1, PAIRS - 1)
            normalise_out(BATCH - 1, PAIRS - 1)
            dve.wait_ge(att_added, PAIRS * BATCH)
            for t in range(TB):
                ln_stats(1, BATCH - 1, acc, t)
            ln_moments(1, BATCH - 1)
            dve.wait_ge(res_ready, BATCH)
            ln_apply(1, BATCH - 1, acc)
            for t in range(TB):
                h1_lo_part(BATCH - 1, t)
            for group, bank, _ in straight(AFTER, (("L", 2, -2), ("L", 3, -2))):
                group_lo(group, bank, BATCH)

        @block.gpsimd
        def _(pool):
            def rstd(n, b):
                pool.wait_ge(var_done[n], b + 1)
                nc.gpsimd.tensor_tensor(ln[n]["rstd"][:], ln[n]["var"][:], half[:], ALU.pow).then_inc(rstd_done[n], 1)

            def add_bv(b):
                pool.wait_ge(acc_loaded, 16 * (b + 1))
                nc.gpsimd.tensor_tensor(acc[:], acc[:], bv_rows[:].unsqueeze(1).to_broadcast([P, TB, DIM]),
                                        ALU.add).then_inc(acc_biased, 1)

            def add_attention(b, p):
                pool.wait_ge(att_done, PAIRS * b + p + 1)
                if p == 0:
                    pool.wait_ge(acc_biased, b + 1)
                cols = slice(P * p, P * p + P)
                nc.gpsimd.tensor_tensor(acc[:, :, cols], acc[:, :, cols], att[:], ALU.add).then_inc(att_added, 1)

            def add_bias(b):
                pool.wait_ge(att_added, PAIRS * (b + 1))
                pool.wait_ge(res_free, 16 + 16 * TB * b)
                nc.gpsimd.tensor_tensor(res[:], acc[:], b1_rows[:].unsqueeze(1).to_broadcast([P, TB, DIM]),
                                        ALU.add).then_inc(res_ready, 1)

            def batch(b, first=False, last=False):
                if not first:
                    add_attention(b - 1, PAIRS - 1)
                    add_bias(b - 1)
                    rstd(1, b - 1)
                    add_bv(b)
                add_attention(b, 0)
                if not last:
                    rstd(0, b + 1)
                add_attention(b, 1)
                add_attention(b, 2)

            nc.gpsimd.memset(ident[:], 0.0).then_inc(consts_ready, 1)
            pool.wait_ge(consts_ready, 2)
            nc.gpsimd.affine_select(out=ident[:], in_=ident[:], compare_op=ALU.not_equal, fill=1.0, base=0,
                                    pattern=[[-1, P]], channel_multiplier=1).then_inc(ident_ready, 1)
            rstd(0, 0)
            pool.wait_ge(deg_step, 3)
            nc.gpsimd.tensor_tensor(dis[:], deg[:], half[:], ALU.pow).then_inc(deg_pow, 1)
            pool.wait_ge(rows_loaded, 16)
            add_bv(0)
            batch(0, first=True)
            with pool.Fori(1, BATCH - 1) as b:
                batch(b)
            batch(BATCH - 1, last=True)
            add_attention(BATCH - 1, PAIRS - 1)
            add_bias(BATCH - 1)
            rstd(1, BATCH - 1)


_INS = ['x', 'adj', 'L0_gnn_Wq', 'L0_gnn_bq', 'L0_gnn_Wk', 'L0_gnn_bk', 'L0_gnn_Wv', 'L0_gnn_bv',
        'L1_gnn_weight', 'L1_gnn_bias']


def kernel(**inputs):
    import numpy as _np
    import concourse.bacc as _bacc
    from concourse import mybir as _mybir
    from concourse.bass_utils import run_bass_kernel_spmd as _run

    nc = _bacc.Bacc("TRN2", target_bir_lowering=False, num_devices=1, dynamic_dma_scratch_size=1024)
    arrays, args = {}, []
    for name in _INS:
        a = _np.ascontiguousarray(inputs[name])
        arrays[f"in_{name}_dram"] = a
        args.append(nc.dram_tensor(f"in_{name}_dram", a.shape, _mybir.dt.from_np(a.dtype), kind="ExternalInput").ap())
    out = nc.dram_tensor("out_dram", (BATCH, TOK, DIM), _mybir.dt.float32, kind="ExternalOutput").ap()
    gnn_layers(nc, *args, out)
    r = _run(nc, [arrays], core_ids=[0])
    return r.results[0]["out_dram"]
```

```python
from contextlib import ExitStack

import concourse.bass as bass
from concourse import mybir

BATCH, TOK, DIM = 32, 512, 512
HEADS, HD = 8, 64
P = 128
TB = TOK // P
CB = DIM // P
PAIRS = HEADS // 2
GB = HEADS * TB
EPS = 1e-5
HI, LO = 0, 1
TERMS = ((HI, HI), (HI, LO), (LO, HI))
SCALE = HD ** -0.5
MASKED = 1e9

F32 = mybir.dt.float32
F32R = mybir.dt.float32r
ALU = mybir.AluOpType
ACT = mybir.ActivationFunctionType
AX_X = mybir.AxisListType.X

ORDER = (
    ("K", 1, 0), ("Q", 1, 0), ("K", 2, 0), ("V", 2, 0), ("Q", 2, 0), ("V", 3, 0), ("K", 3, 0), ("Q", 3, 0),
    ("G", 0, -1), ("G", 1, -1), ("X", 0, 1), ("G", 2, -1), ("X", 1, 1), ("G", 3, -1), ("X", 2, 1),
    ("L", 0, -1), ("X", 3, 1), ("L", 1, -1), ("K", 0, 1), ("Q", 0, 1),
    ("L", 2, -1), ("L", 3, -1), ("V", 0, 1), ("V", 1, 1),
)
PARTS = (3, 3, 2, 3, 2, 3, 2, 3, 2, 2, 2, 3, 3, 3, 2, 2,
         3, 2, 3, 2, 3, 2, 3, 3, 3, 3, 3, 3, 3, 3, 3, 2)
X1_STATS = ((1, 1), (1, 1), (1, 1), (1, 2))
X1_APPLY = ((1, 3), (2, 0), (2, 0), (2, 1))
X1_HI = ((2, 0), (2, 1), (2, 1), (2, 2))
X1_LO = ((2, 1), (2, 2), (2, 2), (2, 3))
X_STATS = ((0, 0), (0, 0), (0, 0), (0, 3))
X_APPLY = ((3, 1), (3, 1), (3, 2), (3, 2))
BEFORE = tuple(("X", c, 0) for c in range(CB)) + tuple(("A", m, 0) for m in range(TB)) + (
    ("K", 0, 0), ("Q", 0, 0), ("V", 0, 0), ("V", 1, 0))
AFTER = tuple(("G", i, -1) for i in range(CB)) + tuple(("L", n, -1) for n in range(TB))


def parts(group):
    return (None,) if group[0] in "XA" else tuple(range(4))


def quarters(first, last):
    run = [("V", 0, 0), ("V", 1, 0)]
    flat = []
    for g in ORDER:
        there = not (first and g[2] < 0) and not (last and g[2] > 0)
        flat += [(g, len(run) % 2, run[-2], c, c == parts(g)[-1]) if there else None for c in parts(g)]
        if there:
            run.append(g)
    assert len(flat) == sum(PARTS) and len(PARTS) == HEADS * TB
    starts = [sum(PARTS[:n]) for n in range(len(PARTS) + 1)]
    mine = [[x for x in flat[starts[n]:starts[n + 1]] if x] for n in range(len(PARTS))]
    return [mine[TB * h:TB * h + TB] for h in range(HEADS)]


def soon(todo, h, q):
    return todo[h][q][:1] if todo[h][q] and todo[h][q][0][4] else []


def late(todo, h, q):
    return todo[h][q][len(soon(todo, h, q)):]


def straight(names, before):
    run = list(before)
    out = []
    for g in names:
        out += [(g, len(run) % 2, run[-2], c, c == parts(g)[-1]) for c in parts(g)]
        run.append(g)
    return out


def gnn_layers(nc, x, adj, wq, bq, wk, bk, wv, bv, w1, b1, out):
    with ExitStack() as ctx:
        def sb(name, shape, dt=F32):
            return ctx.enter_context(nc.sbuf_tensor(name, shape, dt))

        def bank(name):
            return ctx.enter_context(nc.psum_tensor(name, [P, 512], F32))

        def sem(name):
            return ctx.enter_context(nc.semaphore(name))

        WK = sb("WK", [P, 2, CB, DIM], F32R)
        WQ = sb("WQ", [P, 2, CB, DIM], F32R)
        WV = sb("WV", [P, 2, CB, DIM], F32R)
        W1 = sb("W1", [P, 2, CB, DIM], F32R)
        AT = sb("AT", [P, 2, TB, TOK], F32R)
        mask = sb("mask", [P, TB, TOK])
        bv_rows = sb("bv_rows", [P, DIM])
        b1_rows = sb("b1_rows", [P, DIM])
        bk_cols = sb("bk_cols", [P, PAIRS])
        bq_cols = sb("bq_cols", [P, PAIRS])
        ident = sb("ident", [P, P])
        hn = sb("hn", [P, TB, DIM])
        hT = sb("hT", [P, 2, CB, TOK], F32R)
        QS = sb("QS", [P, 2, 2, TOK], F32R)
        KS = sb("KS", [P, 2, 2, 2, TOK], F32R)
        VS = sb("VS", [P, TB, HEADS, 2, HD], F32R)
        probs = sb("probs", [P, 2, TB, TOK])
        PT = sb("PT", [P, TB, 2, TOK], F32R)
        osum = sb("osum", [P, TB, P])
        acc = sb("acc", [P, TB, DIM])
        res = sb("res", [P, TB, DIM])
        H1 = sb("H1", [P, 2, CB, TB, P], F32R)
        nmin = sb("nmin", [P, HEADS, TB])
        sums = sb("sums", [P, HEADS, TB])
        half = sb("half", [P, TB])
        deg = sb("deg", [P, TB])
        dpos = sb("dpos", [P, TB])
        dis = sb("dis", [P, TB])
        ln = [dict(stats=sb(f"stats{n}", [P, TB, 6]), mv=sb(f"mv{n}", [P, TB, 2]),
                   var=sb(f"var{n}", [P, TB]), rstd=sb(f"rstd{n}", [P, TB])) for n in range(2)]

        score_bank = [bank(f"score_bank{i}") for i in range(2)]
        turn_bank = [bank(f"turn_bank{i}") for i in range(2)]
        group_bank = [bank(f"group_bank{i}") for i in range(2)]
        o_bank = [bank(f"o_bank{i}") for i in range(2)]

        x_loaded, acc_loaded = sem("x_loaded"), sem("acc_loaded")
        adj_loaded, cols_loaded, rows_loaded = sem("adj_loaded"), sem("cols_loaded"), sem("rows_loaded")
        wk_loaded, wq_loaded, wv_loaded, w1_loaded = (sem(f"w{n}_loaded") for n in "kqv1")
        k_doubled = [sem(f"k_doubled{i}") for i in range(2)]
        res_free = sem("res_free")
        consts_ready, ident_ready, w_hi, w_split = sem("consts_ready"), sem("ident_ready"), sem("w_hi"), sem("w_split")
        w_scaled, bq_scaled = sem("w_scaled"), sem("bq_scaled")
        deg_step, deg_pow, dis_ready, adj_scaled, mask_ready = (
            sem(n) for n in ("deg_step", "deg_pow", "dis_ready", "adj_scaled", "mask_ready"))
        psum_ready = {k: sem(f"{k}_psum") for k in "XAKQVGL"}
        hi_ready = {k: sem(f"{k}_hi") for k in "XAKQVG"}
        done = {k: sem(f"{k}_done") for k in "XAKQVGL"}
        dve_gate = sem("dve_gate")
        stats_done = [sem(f"stats_done{n}") for n in range(2)]
        moments_done = [sem(f"moments_done{n}") for n in range(2)]
        var_done = [sem(f"var_done{n}") for n in range(2)]
        rstd_done = [sem(f"rstd_done{n}") for n in range(2)]
        normed = [sem(f"normed{n}") for n in range(2)]
        h1_hi, h1_done = sem("h1_hi"), sem("h1_done")
        scores_ready, masked, exp_done = sem("scores_ready"), sem("masked"), sem("exp_done")
        turned, pt_hi, pt_done, pv_done = sem("turned"), sem("pt_hi"), sem("pt_done"), sem("pv_done")
        o_lower, o_done = sem("o_lower"), sem("o_done")
        o_turned, rsums_done, att_done, att_added = sem("o_turned"), sem("rsums_done"), sem("att_done"), sem("att_added")
        acc_biased, res_ready = sem("acc_biased"), sem("res_ready")

        def need(eng, s, count):
            if not isinstance(count, int) or count > 0:
                eng.wait_ge(s, count)

        def nth(group, b):
            kind, i, db = group
            return 4 * (b + db) + i + 1

        x_rows = x.rearrange("b (t p) d -> b p t d", p=P)
        out_rows = out.rearrange("b (t p) d -> b p t d", p=P)

        block = ctx.enter_context(nc.Block())

        @block.sync
        def _(sp):
            sp.dma_start(hn[:], x_rows[0]).then_inc(x_loaded, 16)
            sp.dma_start(probs[:, 0], wk.rearrange("(c p) n -> p c n", p=P)).then_inc(wk_loaded, 16)
            sp.dma_start(probs[:, 1], wq.rearrange("(c p) n -> p c n", p=P)).then_inc(wq_loaded, 16)
            sp.dma_start(bk_cols[:], bk.rearrange("(c p) -> p c", p=P), allow_slow_non_contiguous=True).then_inc(cols_loaded, 16)
            sp.dma_start(bq_cols[:], bq.rearrange("(c p) -> p c", p=P), allow_slow_non_contiguous=True).then_inc(cols_loaded, 16)
            sp.dma_start(mask[:], adj.rearrange("(t p) n -> p t n", p=P)).then_inc(adj_loaded, 16)
            sp.dma_start(acc[:], wv.rearrange("(c p) n -> p c n", p=P)).then_inc(wv_loaded, 16)
            sp.dma_start(res[:], w1.rearrange("(c p) n -> p c n", p=P)).then_inc(w1_loaded, 16)
            sp.dma_start(bv_rows[:], bv.partition_broadcast(P)).then_inc(rows_loaded, 16)
            sp.dma_start(b1_rows[:], b1.partition_broadcast(P)).then_inc(res_free, 16)

            def double_k(b, p):
                sp.wait_ge(done["K"], 4 * b + p + 1)
                sp.dma_start(KS[HD:P, p % 2, 0].bitcast(F32), KS[0:HD, p % 2, 0].bitcast(F32)).then_inc(k_doubled[p % 2], 16)
                sp.dma_start(KS[0:HD, p % 2, 1].bitcast(F32), KS[HD:P, p % 2, 1].bitcast(F32)).then_inc(k_doubled[p % 2], 16)

            def load_acc(b):
                for t in range(TB):
                    need(sp, h1_done, TB * (b - 1) + t + 1)
                    sp.dma_start(acc[:, t], x_rows[b, :, t]).then_inc(acc_loaded, 16)

            def store(b):
                for n in range(TB):
                    sp.wait_ge(done["L"], 4 * b + n + 1)
                    sp.dma_start(out_rows[b, :, n], res[:, n]).then_inc(res_free, 16)

            def batch(b, first=False, last=False):
                if not last:
                    sp.wait_ge(psum_ready["X"], CB * (b + 1))
                    sp.dma_start(hn[:], x_rows[b + 1]).then_inc(x_loaded, 16)
                double_k(b, 1)
                double_k(b, 2)
                if not first:
                    load_acc(b)
                double_k(b, 3)
                if not last:
                    double_k(b + 1, 0)
                if not first:
                    store(b - 1)

            sp.wait_ge(w_split, 3)
            load_acc(0)
            double_k(0, 0)
            batch(0, first=True)
            with sp.Fori(1, BATCH - 1) as b:
                batch(b)
            batch(BATCH - 1, last=True)
            store(BATCH - 1)
            sp.wait_ge(res_free, 16 + 16 * TB * BATCH)

        @block.tensor
        def _(pe):
            def product(psum, wide, moving, c, stop, cols=slice(0, 512)):
                for n, (l, r) in enumerate(TERMS):
                    mm = nc.tensor.matmul(psum[:, cols], wide(l), moving(r),
                                          start=(c == 0 and n == 0), stop=(stop and n == 2))
                return mm

            def piece(group, bank, before, c, ends, b):
                kind, i, db = group
                psum = group_bank[bank]
                if not c:
                    if before is not None:
                        pe.wait_ge(done[before[0]], nth(before, b))
                    if kind in "KQV":
                        pe.wait_ge(done["X"], CB * (b + db + 1))
                    elif kind == "X":
                        pe.wait_ge(normed[0], TB * (b + db + 1))
                    elif kind == "A":
                        pe.wait_ge(adj_scaled, 1)
                    elif kind == "G":
                        pe.wait_ge(h1_done, TB * (b + db + 1))
                    elif kind == "L":
                        pe.wait_ge(done["G"], CB * (b + db + 1))
                if kind in "KQ":
                    w = WK if kind == "K" else WQ
                    mm = product(psum, lambda s: w[:, s, c, P * i:P * i + P], lambda s: hT[:, s, c], c, ends)
                elif kind == "V":
                    j = 2 * (i % 2) + c // 2
                    cols = slice(256 * (c // 2), 256 * (c // 2) + 256)
                    for k in (2 * (c % 2), 2 * (c % 2) + 1):
                        mm = product(psum, lambda s: hT[:, s, k, P * j:P * j + P],
                                     lambda s: WV[:, s, k, 256 * (i // 2):256 * (i // 2) + 256], k, k == CB - 1, cols)
                elif kind == "G":
                    mm = product(psum, lambda s: H1[:, s, i, c], lambda s: AT[:, s, c], c, ends)
                elif kind == "L":
                    mm = product(psum, lambda s: H1[:, s, c, i], lambda s: W1[:, s, c], c, ends)
                else:
                    src = hn if kind == "X" else res
                    for t in range(TB):
                        mm = nc.tensor.transpose(psum[:, P * t:P * t + P], src[:, t, P * i:P * i + P], ident[:])
                if ends:
                    mm.then_inc(psum_ready[kind], 1)

            def scores(b, h, i):
                g, pair = GB * b + TB * h + i, h // 2
                if i == 0 and h % 2 == 0:
                    pe.wait_ge(done["Q"], PAIRS * b + pair + 1)
                    pe.wait_ge(k_doubled[pair % 2], 32 * (PAIRS // 2 * b + pair // 2 + 1))
                need(pe, exp_done, g - 1)
                for s in (HI, LO):
                    mm = nc.tensor.matmul(score_bank[i % 2][:], QS[:, pair % 2, h % 2, P * i:P * i + P],
                                          KS[:, pair % 2, h % 2, s], start=(s == HI), stop=(s == LO))
                mm.then_inc(scores_ready, 1)

            def turn(b, h, j):
                k = GB * b + TB * h + j
                if j == 0:
                    pe.wait_ge(exp_done, GB * b + TB * (h + 1))
                need(pe, pt_done, k - 1)
                for i in range(TB):
                    mm = nc.tensor.transpose(turn_bank[j % 2][:, P * i:P * i + P],
                                             probs[:, h % 2, i, P * j:P * j + P], ident[:])
                mm.then_inc(turned, 1)

            def weigh(b, h, j):
                k = GB * b + TB * h + j
                if j == 0:
                    if h % 2 == 0:
                        need(pe, o_done, HEADS * b + h - 1)
                    else:
                        need(pe, att_done, PAIRS * b + h // 2)
                    if h % 4 == 0:
                        pe.wait_ge(done["V"], 4 * b + 2 * (h // 4) + 2)
                pe.wait_ge(pt_done, k + 1)
                for s in (HI, LO):
                    mm = nc.tensor.matmul(o_bank[h % 2][:], VS[:, j, h].rearrange("p s d -> p (s d)"), PT[:, j, s],
                                          start=(j == 0 and s == HI), stop=(j == TB - 1 and s == LO))
                mm.then_inc(pv_done, 1)

            def turn_out(b, p):
                pe.wait_ge(o_done, HEADS * b + 2 * p + 2)
                for i in range(TB):
                    mm = nc.tensor.transpose(o_bank[1][:, P * i:P * i + P], osum[:, i], ident[:])
                mm.then_inc(o_turned, 1)

            def batch(b, first=False, last=False):
                todo = quarters(first, last)
                for h in range(HEADS):
                    for q in range(TB):
                        if h + 1 < HEADS:
                            scores(b, h + 1, q)
                        elif not last:
                            scores(b + 1, 0, q)
                        for part in todo[h][q]:
                            piece(*part, b)
                        turn(b, h, q)
                        if q > 1:
                            weigh(b, h, q - 2)
                        elif h > 0:
                            weigh(b, h - 1, q + 2)
                        elif not first:
                            weigh(b - 1, HEADS - 1, q + 2)
                        if q == 3 and h % 2 == 0:
                            if h > 0:
                                turn_out(b, h // 2 - 1)
                            elif not first:
                                turn_out(b - 1, PAIRS - 1)

            pe.wait_ge(ident_ready, 1)
            for part in straight(BEFORE, (None, None)):
                if part[0] in (("K", 0, 0), ("Q", 0, 0), ("V", 0, 0)):
                    pe.wait_ge(w_split, {"K": 1, "Q": 2, "V": 3}[part[0][0]])
                piece(*part, 0)
            for q in range(TB):
                scores(0, 0, q)
            pe.wait_ge(w_split, 4)
            pe.wait_ge(done["A"], TB)
            batch(0, first=True)
            with pe.Fori(1, BATCH - 1) as b:
                batch(b)
            batch(BATCH - 1, last=True)
            weigh(BATCH - 1, HEADS - 1, TB - 2)
            weigh(BATCH - 1, HEADS - 1, TB - 1)
            turn_out(BATCH - 1, PAIRS - 1)
            for part in straight(AFTER, (("L", 2, -2), ("L", 3, -2))):
                piece(*part, BATCH)

        @block.scalar
        def _(act):
            def split_hi(w, raw, s, count):
                act.wait_ge(s, count)
                nc.scalar.copy(w[:, HI], raw).then_inc(w_hi, 1)

            def group_hi(group, bank, before, c, ends, b):
                kind, i, db = group
                psum = group_bank[bank]
                if kind == "L" or not ends:
                    return
                act.wait_ge(psum_ready[kind], nth(group, b))
                if kind in "KQ":
                    need(act, scores_ready, 2 * TB * (PAIRS * (b + db) + i - 1))
                    for e in range(2):
                        rows = slice(HD * e, HD * e + HD)
                        to = KS[rows, i % 2, e, HI] if kind == "K" else QS[rows, i % 2, e]
                        cols = bk_cols if kind == "K" else bq_cols
                        last = nc.scalar.activation(to, psum[rows, :], ACT.Identity, bias=cols[rows, i:i + 1])
                        if e == 0:
                            last.then_inc(hi_ready[kind], 1)
                elif kind == "V":
                    need(act, pv_done, GB * (b + db - 1) + GB // 2 * (i // 2 + 1))
                    j, h = 2 * (i % 2), HEADS // 2 * (i // 2)
                    last = nc.scalar.copy(VS[:, j:j + 2, h:h + 4, HI],
                                          psum[:].rearrange("p (j h d) -> p j h d", j=2, d=HD))
                elif kind == "X":
                    last = nc.scalar.activation(hT[:, HI, i], psum[:], ACT.Relu)
                elif kind == "G":
                    last = nc.scalar.copy(H1[:, HI, i].rearrange("p t n -> p (t n)"), psum[:])
                elif kind == "A":
                    last = nc.scalar.mul(AT[:, HI, i], psum[:], dis[:, i:i + 1])
                last.then_inc(hi_ready[kind], 1)

            def exponent(b, h, i):
                g = GB * b + TB * h + i
                act.wait_ge(masked, g + 1)
                if i == 0:
                    need(act, turned, TB * (HEADS * b + h - 1))
                nc.scalar.activation(probs[:, h % 2, i], score_bank[i % 2][:], ACT.Exp, scale=-1.0,
                                     bias=nmin[:, h, i:i + 1], accum_out=sums[:, h, i:i + 1]).then_inc(exp_done, 1)

            def pt_hi_part(b, h, j):
                k = GB * b + TB * h + j
                act.wait_ge(turned, k + 1)
                need(act, pv_done, k - 3)
                nc.scalar.copy(PT[:, j, HI], turn_bank[j % 2][:]).then_inc(pt_hi, 1)

            def o_lower_half(b, h):
                act.wait_ge(pv_done, GB * b + TB * (h + 1))
                need(act, att_added, PAIRS * b + h // 2)
                rows = slice(HD * (h % 2), HD * (h % 2) + HD)
                nc.scalar.copy(osum[rows].rearrange("p i n -> p (i n)"), o_bank[h % 2][HD:P, :]).then_inc(o_lower, 1)

            def h1_hi_part(b, t):
                act.wait_ge(normed[1], TB * b + t + 1)
                nc.scalar.activation(H1[:, HI, :, t], acc[:, t].rearrange("p (c n) -> p c n", n=P),
                                     ACT.Relu).then_inc(h1_hi, 1)

            def batch(b, first=False, last=False):
                todo = quarters(first, last)
                for h in range(HEADS):
                    for q in range(TB):
                        if q == 2:
                            if h > 0:
                                o_lower_half(b, h - 1)
                            elif not first:
                                o_lower_half(b - 1, HEADS - 1)
                        if q > 0:
                            pt_hi_part(b, h, q - 1)
                        elif h > 0:
                            pt_hi_part(b, h - 1, TB - 1)
                        elif not first:
                            pt_hi_part(b - 1, HEADS - 1, TB - 1)
                        for part in soon(todo, h, q):
                            group_hi(*part, b)
                        for t in range(TB):
                            if not first and X1_HI[t] == (h, q):
                                h1_hi_part(b - 1, t)
                        if h + 1 < HEADS:
                            exponent(b, h + 1, q)
                        elif not last:
                            exponent(b + 1, 0, q)
                        for part in late(todo, h, q):
                            group_hi(*part, b)

            split_hi(WK, probs[:, 0], wk_loaded, 16)
            split_hi(WQ, probs[:, 1], w_scaled, 1)
            split_hi(WV, acc[:], wv_loaded, 16)
            split_hi(W1, res[:], w1_loaded, 16)
            act.wait_ge(bq_scaled, 1)
            act.wait_ge(cols_loaded, 32)
            act.wait_ge(dis_ready, 1)
            for part in straight(BEFORE, (None, None)):
                group_hi(*part, 0)
            act.wait_ge(w_split, 2)
            for q in range(TB):
                exponent(0, 0, q)
            batch(0, first=True)
            with act.Fori(1, BATCH - 1) as b:
                batch(b)
            batch(BATCH - 1, last=True)
            pt_hi_part(BATCH - 1, HEADS - 1, TB - 1)
            o_lower_half(BATCH - 1, HEADS - 1)
            for t in range(TB):
                h1_hi_part(BATCH - 1, t)
            for part in straight(AFTER, (("L", 2, -2), ("L", 3, -2))):
                group_hi(*part, BATCH)

        @block.vector
        def _(dve):
            def split_lo(w, raw, count):
                dve.wait_ge(w_hi, count)
                nc.vector.tensor_tensor(w[:, LO], raw, w[:, HI].bitcast(F32), ALU.subtract).then_inc(w_split, 1)

            def group_lo(group, bank, before, c, ends, b):
                kind, i, db = group
                psum = group_bank[bank]
                if not ends:
                    return
                if kind == "L":
                    dve.wait_ge(psum_ready["L"], nth(group, b))
                    last = nc.vector.tensor_tensor(res[:, i], psum[:], res[:, i], ALU.add)
                elif kind not in "KQ":
                    dve.wait_ge(hi_ready[kind], nth(group, b))
                if kind in "KQ":
                    for e in range(2):
                        dve.wait_ge(hi_ready[kind], 2 * nth(group, b) - 1 + e)
                        rows, other = slice(HD * e, HD * e + HD), slice(HD * (1 - e), HD * (1 - e) + HD)
                        hi = KS[rows, i % 2, e, HI] if kind == "K" else QS[rows, i % 2, e]
                        lo = KS[rows, i % 2, e, LO] if kind == "K" else QS[other, i % 2, e]
                        cols = bk_cols if kind == "K" else bq_cols
                        last = nc.vector.scalar_tensor_tensor(lo, psum[rows, :], cols[rows, i:i + 1],
                                                              hi.bitcast(F32), ALU.add, ALU.subtract)
                elif kind == "V":
                    j, h = 2 * (i % 2), HEADS // 2 * (i // 2)
                    last = nc.vector.tensor_tensor(VS[:, j:j + 2, h:h + 4, LO],
                                                   psum[:].rearrange("p (j h d) -> p j h d", j=2, d=HD),
                                                   VS[:, j:j + 2, h:h + 4, HI].bitcast(F32), ALU.subtract)
                elif kind == "X":
                    last = nc.vector.scalar_tensor_tensor(hT[:, LO, i], psum[:], 0.0, hT[:, HI, i].bitcast(F32),
                                                          ALU.max, ALU.subtract)
                elif kind == "G":
                    last = nc.vector.tensor_tensor(H1[:, LO, i].rearrange("p t n -> p (t n)"), psum[:],
                                                   H1[:, HI, i].rearrange("p t n -> p (t n)").bitcast(F32),
                                                   ALU.subtract)
                elif kind == "A":
                    last = nc.vector.scalar_tensor_tensor(AT[:, LO, i], psum[:], dis[:, i:i + 1],
                                                          AT[:, HI, i].bitcast(F32), ALU.mult, ALU.subtract)
                last.then_inc(done[kind], 1)

            def mask_scores(b, h, i):
                dve.wait_ge(scores_ready, GB * b + TB * h + i + 1)
                nc.vector.sem_inc(dve_gate, 1)
                nc.vector.tensor_tensor_reduce(score_bank[i % 2][:], score_bank[i % 2][:], mask[:, i], 1.0, 3.4e38,
                                               ALU.add, ALU.min, nmin[:, h, i:i + 1]).then_inc(masked, 1)

            def pt_lo_part(b, h, j):
                dve.wait_ge(pt_hi, GB * b + TB * h + j + 1)
                nc.vector.tensor_tensor(PT[:, j, LO], turn_bank[j % 2][:], PT[:, j, HI].bitcast(F32),
                                        ALU.subtract).then_inc(pt_done, 1)

            def o_add(b, h):
                dve.wait_ge(o_lower, HEADS * b + h + 1)
                rows = slice(HD * (h % 2), HD * (h % 2) + HD)
                both = osum[rows].rearrange("p i n -> p (i n)")
                nc.vector.tensor_tensor(both, o_bank[h % 2][0:HD, :], both, ALU.add).then_inc(o_done, 1)

            def invert_sums(b, p):
                dve.wait_ge(exp_done, 2 * TB * (PAIRS * b + p + 1))
                nc.vector.reciprocal(sums[:, 2 * p:2 * p + 2], sums[:, 2 * p:2 * p + 2]).then_inc(rsums_done, 1)

            def normalise_out(b, p):
                dve.wait_ge(rsums_done, PAIRS * b + p + 1)
                dve.wait_ge(o_turned, PAIRS * b + p + 1)
                nc.vector.tensor_tensor(
                    osum[:].rearrange("p i (h d) -> p i h d", d=HD),
                    o_bank[1][:].rearrange("p (i h d) -> p i h d", i=TB, d=HD),
                    sums[:, 2 * p:2 * p + 2].rearrange("p h i -> p i h").unsqueeze(3).to_broadcast([P, TB, 2, HD]),
                    ALU.mult).then_inc(att_done, 1)

            def ln_stats(n, b, src, t):
                nc.vector.bn_stats(ln[n]["stats"][:, t], src[:, t]).then_inc(stats_done[n], 1)

            def ln_moments(n, b):
                for t in range(TB):
                    if t == 0:
                        dve.wait_ge(stats_done[n], TB * (b + 1))
                        nc.vector.sem_inc(dve_gate, 1)
                    nc.vector.bn_aggr(ln[n]["mv"][:, t], ln[n]["stats"][:, t]).then_inc(moments_done[n], 1)
                dve.wait_ge(moments_done[n], TB * (b + 1))
                nc.vector.tensor_scalar(ln[n]["var"][:], ln[n]["mv"][:, :, 1], EPS, None, ALU.add).then_inc(var_done[n], 1)

            def ln_apply(n, b, src, t):
                if t == 0:
                    dve.wait_ge(rstd_done[n], b + 1)
                nc.vector.tensor_scalar(src[:, t], src[:, t], ln[n]["mv"][:, t, 0:1], ln[n]["rstd"][:, t:t + 1],
                                        ALU.subtract, ALU.mult).then_inc(normed[n], 1)

            def h1_lo_part(b, t):
                dve.wait_ge(h1_hi, TB * b + t + 1)
                nc.vector.scalar_tensor_tensor(H1[:, LO, :, t], acc[:, t].rearrange("p (c n) -> p c n", n=P), 0.0,
                                               H1[:, HI, :, t].bitcast(F32), ALU.max, ALU.subtract).then_inc(h1_done, 1)

            def batch(b, first=False, last=False):
                todo = quarters(first, last)
                for h in range(HEADS):
                    for q in range(TB):
                        if h + 1 < HEADS:
                            mask_scores(b, h + 1, q)
                        elif not last:
                            mask_scores(b + 1, 0, q)
                        if q > 0:
                            pt_lo_part(b, h, q - 1)
                        elif h > 0:
                            pt_lo_part(b, h - 1, TB - 1)
                        elif not first:
                            pt_lo_part(b - 1, HEADS - 1, TB - 1)
                        for part in soon(todo, h, q):
                            group_lo(*part, b)
                        if q == 2:
                            if h > 0:
                                o_add(b, h - 1)
                            elif not first:
                                o_add(b - 1, HEADS - 1)
                        if h % 2 == 1 and (h > 1 or not first):
                            bb, p = (b, h // 2 - 1) if h > 1 else (b - 1, PAIRS - 1)
                            if q == 0:
                                invert_sums(bb, p)
                                normalise_out(bb, p)
                        if not first:
                            ln_x1(b - 1, h, q)
                        if not last:
                            ln_x(b + 1, h, q)
                        for part in late(todo, h, q):
                            group_lo(*part, b)

            def ln_x1(b, h, q):
                for t in range(TB):
                    if X1_STATS[t] == (h, q):
                        if t == 0:
                            dve.wait_ge(att_added, PAIRS * (b + 1))
                        ln_stats(1, b, acc, t)
                        if t == TB - 1:
                            ln_moments(1, b)
                    if X1_APPLY[t] == (h, q):
                        if t == 0:
                            dve.wait_ge(res_ready, b + 1)
                        ln_apply(1, b, acc, t)
                    if X1_LO[t] == (h, q):
                        h1_lo_part(b, t)

            def ln_x(b, h, q):
                for t in range(TB):
                    if X_STATS[t] == (h, q):
                        if t == 0:
                            dve.wait_ge(x_loaded, 16 * (b + 1))
                        ln_stats(0, b, hn, t)
                        if t == TB - 1:
                            ln_moments(0, b)
                    if X_APPLY[t] == (h, q):
                        ln_apply(0, b, hn, t)

            nc.vector.memset(half[:], -0.5).then_inc(consts_ready, 1)
            dve.wait_ge(x_loaded, 16)
            for t in range(TB):
                ln_stats(0, 0, hn, t)
            ln_moments(0, 0)
            dve.wait_ge(wq_loaded, 16)
            nc.vector.tensor_scalar(probs[:, 1], probs[:, 1], -SCALE, None, ALU.mult).then_inc(w_scaled, 1)
            dve.wait_ge(cols_loaded, 32)
            nc.vector.tensor_scalar(bq_cols[:], bq_cols[:], -SCALE, None, ALU.mult).then_inc(bq_scaled, 1)
            for t in range(TB):
                ln_apply(0, 0, hn, t)
            dve.wait_ge(adj_loaded, 16)
            nc.vector.tensor_reduce(deg[:], mask[:], AX_X, ALU.add).then_inc(deg_step, 1)
            dve.wait_ge(deg_step, 1)
            nc.vector.tensor_scalar(dpos[:], deg[:], 0.0, None, ALU.is_gt).then_inc(deg_step, 1)
            dve.wait_ge(deg_step, 2)
            nc.vector.tensor_scalar(deg[:], deg[:], 1.1754944e-38, None, ALU.max).then_inc(deg_step, 1)
            split_lo(WK, probs[:, 0], 1)
            split_lo(WQ, probs[:, 1], 2)
            split_lo(WV, acc[:], 3)
            split_lo(W1, res[:], 4)
            dve.wait_ge(deg_pow, 1)
            nc.vector.tensor_tensor(dis[:], dis[:], dpos[:], ALU.mult).then_inc(dis_ready, 1)
            dve.wait_ge(dis_ready, 1)
            dve.wait_ge(w_split, 4)
            for t in range(TB):
                last = nc.vector.tensor_scalar(res[:, t], mask[:, t], dis[:, t:t + 1], None, ALU.mult)
            last.then_inc(adj_scaled, 1)
            dve.wait_ge(adj_scaled, 1)
            nc.vector.tensor_scalar(mask[:], mask[:], 0.0, MASKED, ALU.is_equal, ALU.mult).then_inc(mask_ready, 1)
            for part in straight(BEFORE, (None, None)):
                group_lo(*part, 0)
            dve.wait_ge(mask_ready, 1)
            for q in range(TB):
                mask_scores(0, 0, q)
            batch(0, first=True)
            with dve.Fori(1, BATCH - 1) as b:
                batch(b)
            batch(BATCH - 1, last=True)
            pt_lo_part(BATCH - 1, HEADS - 1, TB - 1)
            o_add(BATCH - 1, HEADS - 1)
            invert_sums(BATCH - 1, PAIRS - 1)
            normalise_out(BATCH - 1, PAIRS - 1)
            dve.wait_ge(att_added, PAIRS * BATCH)
            for t in range(TB):
                ln_stats(1, BATCH - 1, acc, t)
            ln_moments(1, BATCH - 1)
            dve.wait_ge(res_ready, BATCH)
            for t in range(TB):
                ln_apply(1, BATCH - 1, acc, t)
            for t in range(TB):
                h1_lo_part(BATCH - 1, t)
            for part in straight(AFTER, (("L", 2, -2), ("L", 3, -2))):
                group_lo(*part, BATCH)

        @block.gpsimd
        def _(pool):
            def rstd(n, b):
                pool.wait_ge(var_done[n], b + 1)
                nc.gpsimd.tensor_tensor(ln[n]["rstd"][:], ln[n]["var"][:], half[:], ALU.pow).then_inc(rstd_done[n], 1)

            def add_bv(b, p):
                if p == 0:
                    pool.wait_ge(acc_loaded, 16 * TB * (b + 1))
                cols = slice(P * p, P * p + P)
                nc.gpsimd.tensor_tensor(acc[:, :, cols], acc[:, :, cols],
                                        bv_rows[:, cols].unsqueeze(1).to_broadcast([P, TB, P]),
                                        ALU.add).then_inc(acc_biased, 1)

            def add_attention(b, p):
                pool.wait_ge(att_done, PAIRS * b + p + 1)
                pool.wait_ge(acc_biased, PAIRS * b + p + 1)
                cols = slice(P * p, P * p + P)
                nc.gpsimd.tensor_tensor(acc[:, :, cols], acc[:, :, cols], osum[:], ALU.add).then_inc(att_added, 1)

            def add_bias(b):
                pool.wait_ge(att_added, PAIRS * (b + 1))
                pool.wait_ge(res_free, 16 + 16 * TB * b)
                nc.gpsimd.tensor_tensor(res[:], acc[:], b1_rows[:].unsqueeze(1).to_broadcast([P, TB, DIM]),
                                        ALU.add).then_inc(res_ready, 1)

            def batch(b, first=False, last=False):
                if not last:
                    rstd(0, b + 1)
                if not first:
                    add_attention(b - 1, PAIRS - 1)
                    add_bias(b - 1)
                    rstd(1, b - 1)
                add_bv(b, 0)
                add_attention(b, 0)
                add_bv(b, 1)
                add_attention(b, 1)
                add_bv(b, 2)
                add_attention(b, 2)
                add_bv(b, 3)

            nc.gpsimd.memset(ident[:], 0.0).then_inc(consts_ready, 1)
            pool.wait_ge(consts_ready, 2)
            nc.gpsimd.affine_select(out=ident[:], in_=ident[:], compare_op=ALU.not_equal, fill=1.0, base=0,
                                    pattern=[[-1, P]], channel_multiplier=1).then_inc(ident_ready, 1)
            rstd(0, 0)
            pool.wait_ge(deg_step, 3)
            nc.gpsimd.tensor_tensor(dis[:], deg[:], half[:], ALU.pow).then_inc(deg_pow, 1)
            pool.wait_ge(rows_loaded, 16)
            batch(0, first=True)
            with pool.Fori(1, BATCH - 1) as b:
                batch(b)
            batch(BATCH - 1, last=True)
            add_attention(BATCH - 1, PAIRS - 1)
            add_bias(BATCH - 1)
            rstd(1, BATCH - 1)


_INS = ['x', 'adj', 'L0_gnn_Wq', 'L0_gnn_bq', 'L0_gnn_Wk', 'L0_gnn_bk', 'L0_gnn_Wv', 'L0_gnn_bv',
        'L1_gnn_weight', 'L1_gnn_bias']


def kernel(**inputs):
    import numpy as _np
    import concourse.bacc as _bacc
    from concourse import mybir as _mybir
    from concourse.bass_utils import run_bass_kernel_spmd as _run

    nc = _bacc.Bacc("TRN2", target_bir_lowering=False, num_devices=1, dynamic_dma_scratch_size=512)
    arrays, args = {}, []
    for name in _INS:
        a = _np.ascontiguousarray(inputs[name])
        arrays[f"in_{name}_dram"] = a
        args.append(nc.dram_tensor(f"in_{name}_dram", a.shape, _mybir.dt.from_np(a.dtype), kind="ExternalInput").ap())
    out = nc.dram_tensor("out_dram", (BATCH, TOK, DIM), _mybir.dt.float32, kind="ExternalOutput").ap()
    gnn_layers(nc, *args, out)
    r = _run(nc, [arrays], core_ids=[0])
    return r.results[0]["out_dram"]
```

```python
from contextlib import ExitStack

import concourse.bass as bass
from concourse import mybir

BATCH, TOK, DIM = 32, 512, 512
HEADS, HD = 8, 64
P = 128
TB = TOK // P
CB = DIM // P
PAIRS = HEADS // 2
GB = HEADS * TB
EPS = 1e-5
HI, LO = 0, 1
TERMS = ((HI, HI), (HI, LO), (LO, HI))
SCALE = HD ** -0.5
MASKED = 1e9

F32 = mybir.dt.float32
F32R = mybir.dt.float32r
ALU = mybir.AluOpType
ACT = mybir.ActivationFunctionType
AX_X = mybir.AxisListType.X

ORDER = (
    ("K", 1, 0), ("Q", 1, 0), ("K", 2, 0), ("V", 2, 0), ("Q", 2, 0), ("V", 3, 0), ("K", 3, 0), ("Q", 3, 0),
    ("G", 0, -1), ("G", 1, -1), ("G", 2, -1), ("X", 0, 1), ("G", 3, -1), ("X", 1, 1), ("L", 0, -1), ("X", 2, 1),
    ("L", 1, -1), ("X", 3, 1), ("K", 0, 1), ("Q", 0, 1), ("L", 2, -1), ("L", 3, -1), ("V", 0, 1), ("V", 1, 1),
)
PARTS = (3, 3, 2, 3, 2, 3, 2, 3, 2, 2, 2, 3, 3, 3, 3, 2,
         3, 3, 2, 3, 2, 3, 2, 3, 3, 3, 3, 3, 3, 3, 2, 2)
X1_STATS = ((1, 1), (1, 1), (1, 1), (1, 2))
X1_APPLY = ((1, 3), (2, 0), (2, 0), (2, 1))
X1_HI = ((2, 0), (2, 1), (2, 1), (2, 2))
X1_LO = ((2, 1), (2, 2), (2, 2), (2, 3))
X_STATS = ((0, 0), (0, 0), (0, 0), (0, 3))
X_APPLY = ((3, 1), (3, 2), (3, 3), (3, 3))
BEFORE = tuple(zip([("X", c, 0) for c in range(CB)] + [("K", 0, 0), ("Q", 0, 0)]
                   + [("A", m, 0) for m in range(TB)] + [("V", 0, 0), ("V", 1, 0)],
                   (0, 1, 2, 3, 0, 1, 2, 3, 2, 3, 0, 1)))
AFTER = tuple(zip([("G", i, -1) for i in range(CB)] + [("L", n, -1) for n in range(TB)],
                  (0, 1, 2, 3, 0, 1, 2, 3)))


def parts(group):
    return (None,) if group[0] in "XA" else tuple(range(4))


def quarters(first, last):
    run = [("V", 0, 0), ("V", 1, 0)]
    flat = []
    for g in ORDER:
        there = not (first and g[2] < 0) and not (last and g[2] > 0)
        flat += [(g, len(run) % 2, run[-2], c, c == parts(g)[-1]) if there else None for c in parts(g)]
        if there:
            run.append(g)
    assert len(flat) == sum(PARTS) and len(PARTS) == HEADS * TB
    starts = [sum(PARTS[:n]) for n in range(len(PARTS) + 1)]
    mine = [[x for x in flat[starts[n]:starts[n + 1]] if x] for n in range(len(PARTS))]
    return [mine[TB * h:TB * h + TB] for h in range(HEADS)]


def soon(todo, h, q):
    return todo[h][q][:1] if todo[h][q] and todo[h][q][0][4] else []


def late(todo, h, q):
    return todo[h][q][len(soon(todo, h, q)):]


def straight(groups, had=()):
    had = dict(had)
    out = []
    for g, bank in groups:
        out += [(g, bank, had.get(bank), c, c == parts(g)[-1]) for c in parts(g)]
        had[bank] = g
    return out


def gnn_layers(nc, x, adj, wq, bq, wk, bk, wv, bv, w1, b1, out):
    with ExitStack() as ctx:
        def sb(name, shape, dt=F32):
            return ctx.enter_context(nc.sbuf_tensor(name, shape, dt))

        def bank(name):
            return ctx.enter_context(nc.psum_tensor(name, [P, 512], F32))

        def sem(name):
            return ctx.enter_context(nc.semaphore(name))

        WK = sb("WK", [P, 2, CB, DIM], F32R)
        WQ = sb("WQ", [P, 2, CB, DIM], F32R)
        WV = sb("WV", [P, 2, CB, DIM], F32R)
        W1 = sb("W1", [P, 2, CB, DIM], F32R)
        AT = sb("AT", [P, 2, TB, TOK], F32R)
        mask = sb("mask", [P, TB, TOK])
        bv_rows = sb("bv_rows", [P, DIM])
        b1_rows = sb("b1_rows", [P, DIM])
        bk_cols = sb("bk_cols", [P, PAIRS])
        bq_cols = sb("bq_cols", [P, PAIRS])
        ident = sb("ident", [P, P])
        hn = sb("hn", [P, TB, DIM])
        hT = sb("hT", [P, 2, CB, TOK], F32R)
        QS = sb("QS", [P, 2, 2, TOK], F32R)
        KS = sb("KS", [P, 2, 2, 2, TOK], F32R)
        VS = sb("VS", [P, TB, HEADS, 2, HD], F32R)
        probs = sb("probs", [P, 2, TB, TOK])
        PT = sb("PT", [P, TB, 2, TOK], F32R)
        osum = sb("osum", [P, TB, P])
        acc = sb("acc", [P, TB, DIM])
        res = sb("res", [P, TB, DIM])
        H1 = sb("H1", [P, 2, CB, TB, P], F32R)
        nmin = sb("nmin", [P, HEADS, TB])
        sums = sb("sums", [P, HEADS, TB])
        half = sb("half", [P, TB])
        deg = sb("deg", [P, TB])
        dpos = sb("dpos", [P, TB])
        dis = sb("dis", [P, TB])
        ln = [dict(stats=sb(f"stats{n}", [P, TB, 6]), mv=sb(f"mv{n}", [P, TB, 2]),
                   var=sb(f"var{n}", [P, TB]), rstd=sb(f"rstd{n}", [P, TB])) for n in range(2)]

        score_bank = [bank(f"score_bank{i}") for i in range(2)]
        turn_bank = [bank(f"turn_bank{i}") for i in range(2)]
        group_bank = [bank(f"group_bank{i}") for i in range(2)]
        o_bank = [bank(f"o_bank{i}") for i in range(2)]

        x_loaded, acc_loaded = sem("x_loaded"), sem("acc_loaded")
        adj_loaded, cols_loaded, rows_loaded = sem("adj_loaded"), sem("cols_loaded"), sem("rows_loaded")
        wk_loaded, wq_loaded, wv_loaded, w1_loaded = (sem(f"w{n}_loaded") for n in "kqv1")
        k_doubled = [sem(f"k_doubled{i}") for i in range(2)]
        res_free = sem("res_free")
        x0_loaded = [sem(f"x0_loaded{t}") for t in range(TB)]
        consts_ready, ident_ready, w_hi, w_split = sem("consts_ready"), sem("ident_ready"), sem("w_hi"), sem("w_split")
        bq_scaled = sem("bq_scaled")
        deg_step, deg_pow, dis_ready, adj_scaled, mask_ready = (
            sem(n) for n in ("deg_step", "deg_pow", "dis_ready", "adj_scaled", "mask_ready"))
        psum_ready = {k: sem(f"{k}_psum") for k in "XAKQVGL"}
        hi_ready = {k: sem(f"{k}_hi") for k in "XAKQVG"}
        done = {k: sem(f"{k}_done") for k in "XAKQVGL"}
        dve_gate = sem("dve_gate")
        stats_done = [sem(f"stats_done{n}") for n in range(2)]
        moments_done = [sem(f"moments_done{n}") for n in range(2)]
        var_done = [sem(f"var_done{n}") for n in range(2)]
        rstd_done = [sem(f"rstd_done{n}") for n in range(2)]
        normed = [sem(f"normed{n}") for n in range(2)]
        h1_hi, h1_done = sem("h1_hi"), sem("h1_done")
        scores_ready, masked, exp_done = sem("scores_ready"), sem("masked"), sem("exp_done")
        turned, pt_hi, pt_done, pv_done = sem("turned"), sem("pt_hi"), sem("pt_done"), sem("pv_done")
        o_lower, o_done = sem("o_lower"), sem("o_done")
        o_turned, rsums_done, att_done, att_added = sem("o_turned"), sem("rsums_done"), sem("att_done"), sem("att_added")
        acc_biased, res_ready = sem("acc_biased"), sem("res_ready")

        def need(eng, s, count):
            if not isinstance(count, int) or count > 0:
                eng.wait_ge(s, count)

        def nth(group, b):
            kind, i, db = group
            return 4 * (b + db) + i + 1

        x_rows = x.rearrange("b (t p) d -> b p t d", p=P)
        out_rows = out.rearrange("b (t p) d -> b p t d", p=P)

        block = ctx.enter_context(nc.Block())

        @block.sync
        def _(sp):
            for t in range(TB):
                sp.dma_start(hn[:, t], x_rows[0, :, t]).then_inc(x0_loaded[t], 16)
            sp.dma_start(probs[:, 0], wk.rearrange("(c p) n -> p c n", p=P)).then_inc(wk_loaded, 16)
            sp.dma_start(probs[:, 1], wq.rearrange("(c p) n -> p c n", p=P)).then_inc(wq_loaded, 16)
            sp.dma_start(bk_cols[:], bk.rearrange("(c p) -> p c", p=P), allow_slow_non_contiguous=True).then_inc(cols_loaded, 16)
            sp.dma_start(bq_cols[:], bq.rearrange("(c p) -> p c", p=P), allow_slow_non_contiguous=True).then_inc(cols_loaded, 16)
            sp.dma_start(mask[:], adj.rearrange("(t p) n -> p t n", p=P)).then_inc(adj_loaded, 16)
            sp.dma_start(acc[:], wv.rearrange("(c p) n -> p c n", p=P)).then_inc(wv_loaded, 16)
            sp.dma_start(res[:], w1.rearrange("(c p) n -> p c n", p=P)).then_inc(w1_loaded, 16)
            sp.dma_start(bv_rows[:], bv.partition_broadcast(P)).then_inc(rows_loaded, 16)
            sp.dma_start(b1_rows[:], b1.partition_broadcast(P)).then_inc(res_free, 16)

            def double_k(b, p):
                sp.wait_ge(done["K"], 4 * b + p + 1)
                sp.dma_start(KS[HD:P, p % 2, 0].bitcast(F32), KS[0:HD, p % 2, 0].bitcast(F32)).then_inc(k_doubled[p % 2], 16)
                sp.dma_start(KS[0:HD, p % 2, 1].bitcast(F32), KS[HD:P, p % 2, 1].bitcast(F32)).then_inc(k_doubled[p % 2], 16)

            def load_acc(b):
                for t in range(TB):
                    need(sp, h1_done, TB * (b - 1) + t + 1)
                    sp.dma_start(acc[:, t], x_rows[b, :, t]).then_inc(acc_loaded, 16)

            def store(b):
                for n in range(TB):
                    sp.wait_ge(done["L"], 4 * b + n + 1)
                    sp.dma_start(out_rows[b, :, n], res[:, n]).then_inc(res_free, 16)

            def batch(b, first=False, last=False):
                if not last:
                    sp.wait_ge(psum_ready["X"], CB * (b + 1))
                    if first:
                        sp.wait_ge(psum_ready["A"], TB)
                    sp.dma_start(hn[:], x_rows[b + 1]).then_inc(x_loaded, 16)
                double_k(b, 1)
                double_k(b, 2)
                if not first:
                    load_acc(b)
                double_k(b, 3)
                if not last:
                    double_k(b + 1, 0)
                if not first:
                    store(b - 1)

            double_k(0, 0)
            sp.wait_ge(w_split, 3)
            load_acc(0)
            batch(0, first=True)
            with sp.Fori(1, BATCH - 1) as b:
                batch(b)
            batch(BATCH - 1, last=True)
            store(BATCH - 1)
            sp.wait_ge(res_free, 16 + 16 * TB * BATCH)

        @block.tensor
        def _(pe):
            def product(psum, wide, moving, c, stop, cols=slice(0, 512)):
                for n, (l, r) in enumerate(TERMS):
                    mm = nc.tensor.matmul(psum[:, cols], wide(l), moving(r),
                                          start=(c == 0 and n == 0), stop=(stop and n == 2))
                return mm

            def piece(group, bank, before, c, ends, b):
                kind, i, db = group
                psum = (group_bank + turn_bank)[bank]
                if (kind, i) == ("K", 0):
                    pe.wait_ge(done["X"], CB * (b + db) + c + 1)
                elif (kind, i) == ("G", 0):
                    pe.wait_ge(h1_done, TB * (b + db) + c + 1)
                elif (kind, i) == ("L", 0):
                    pe.wait_ge(done["G"], CB * (b + db) + c + 1)
                if not c:
                    if before is not None:
                        pe.wait_ge(done[before[0]], nth(before, b))
                    if kind in "KQV" and (kind, i) != ("K", 0):
                        pe.wait_ge(done["X"], CB * (b + db + 1))
                    elif kind == "X":
                        pe.wait_ge(normed[0], TB * (b + db + 1))
                    elif kind == "A":
                        pe.wait_ge(adj_scaled, 1)
                    elif kind == "G" and i:
                        pe.wait_ge(h1_done, TB * (b + db + 1))
                    elif kind == "L" and i:
                        pe.wait_ge(done["G"], CB * (b + db + 1))
                if kind in "KQ":
                    w = WK if kind == "K" else WQ
                    mm = product(psum, lambda s: w[:, s, c, P * i:P * i + P], lambda s: hT[:, s, c], c, ends)
                elif kind == "V":
                    j = 2 * (i % 2) + c // 2
                    cols = slice(256 * (c // 2), 256 * (c // 2) + 256)
                    for k in (2 * (c % 2), 2 * (c % 2) + 1):
                        mm = product(psum, lambda s: hT[:, s, k, P * j:P * j + P],
                                     lambda s: WV[:, s, k, 256 * (i // 2):256 * (i // 2) + 256], k, k == CB - 1, cols)
                elif kind == "G":
                    mm = product(psum, lambda s: H1[:, s, i, c], lambda s: AT[:, s, c], c, ends)
                elif kind == "L":
                    mm = product(psum, lambda s: H1[:, s, c, i], lambda s: W1[:, s, c], c, ends)
                else:
                    for t in range(TB):
                        mm = nc.tensor.transpose(psum[:, P * t:P * t + P], hn[:, t, P * i:P * i + P], ident[:])
                if ends:
                    mm.then_inc(psum_ready[kind], 1)

            def scores(b, h, i):
                g, pair = GB * b + TB * h + i, h // 2
                if i == 0 and h % 2 == 0:
                    pe.wait_ge(done["Q"], PAIRS * b + pair + 1)
                    pe.wait_ge(k_doubled[pair % 2], 32 * (PAIRS // 2 * b + pair // 2 + 1))
                need(pe, exp_done, g - 1)
                for s in (HI, LO):
                    mm = nc.tensor.matmul(score_bank[i % 2][:], QS[:, pair % 2, h % 2, P * i:P * i + P],
                                          KS[:, pair % 2, h % 2, s], start=(s == HI), stop=(s == LO))
                mm.then_inc(scores_ready, 1)

            def turn(b, h, j):
                k = GB * b + TB * h + j
                if j == 0:
                    pe.wait_ge(exp_done, GB * b + TB * (h + 1))
                need(pe, pt_done, k - 1)
                for i in range(TB):
                    mm = nc.tensor.transpose(turn_bank[j % 2][:, P * i:P * i + P],
                                             probs[:, h % 2, i, P * j:P * j + P], ident[:])
                mm.then_inc(turned, 1)

            def weigh(b, h, j):
                k = GB * b + TB * h + j
                if j == 0:
                    if h % 2 == 0:
                        need(pe, o_done, HEADS * b + h - 1)
                    else:
                        need(pe, att_done, PAIRS * b + h // 2)
                    if h % 4 == 0:
                        pe.wait_ge(done["V"], 4 * b + 2 * (h // 4) + 2)
                pe.wait_ge(pt_done, k + 1)
                for s in (HI, LO):
                    mm = nc.tensor.matmul(o_bank[h % 2][:], VS[:, j, h].rearrange("p s d -> p (s d)"), PT[:, j, s],
                                          start=(j == 0 and s == HI), stop=(j == TB - 1 and s == LO))
                mm.then_inc(pv_done, 1)

            def turn_out(b, p):
                pe.wait_ge(o_done, HEADS * b + 2 * p + 2)
                for i in range(TB):
                    mm = nc.tensor.transpose(o_bank[1][:, P * i:P * i + P], osum[:, i], ident[:])
                mm.then_inc(o_turned, 1)

            def batch(b, first=False, last=False):
                todo = quarters(first, last)
                for h in range(HEADS):
                    for q in range(TB):
                        if h + 1 < HEADS:
                            scores(b, h + 1, q)
                        elif not last:
                            scores(b + 1, 0, q)
                        for part in todo[h][q]:
                            piece(*part, b)
                        turn(b, h, q)
                        if q > 1:
                            weigh(b, h, q - 2)
                        elif h > 0:
                            weigh(b, h - 1, q + 2)
                        elif not first:
                            weigh(b - 1, HEADS - 1, q + 2)
                        if q == 3 and h % 2 == 0:
                            if h > 0:
                                turn_out(b, h // 2 - 1)
                            elif not first:
                                turn_out(b - 1, PAIRS - 1)

            pe.wait_ge(ident_ready, 1)
            before = straight(BEFORE)
            for part in before[:CB + 8]:
                if part[0][0] in "KQ" and not part[3]:
                    pe.wait_ge(w_split, "KQ".index(part[0][0]) + 1)
                piece(*part, 0)
            scores(0, 0, 0)
            scores(0, 0, 1)
            for part in before[CB + 8:-4]:
                if part[0] == ("V", 0, 0) and not part[3]:
                    pe.wait_ge(w_split, 3)
                piece(*part, 0)
            scores(0, 0, 2)
            scores(0, 0, 3)
            for part in before[-4:]:
                piece(*part, 0)
            pe.wait_ge(done["A"], TB)
            batch(0, first=True)
            pe.wait_ge(w_split, 4)
            with pe.Fori(1, BATCH - 1) as b:
                batch(b)
            batch(BATCH - 1, last=True)
            weigh(BATCH - 1, HEADS - 1, TB - 2)
            weigh(BATCH - 1, HEADS - 1, TB - 1)
            turn_out(BATCH - 1, PAIRS - 1)
            for part in straight(AFTER, ((0, ("L", 2, -2)), (1, ("L", 3, -2)))):
                piece(*part, BATCH)

        @block.scalar
        def _(act):
            def split_hi(w, raw, loaded, scale=1.0):
                act.wait_ge(loaded, 16)
                nc.scalar.activation(w[:, HI], raw, ACT.Copy, scale=scale).then_inc(w_hi, 1)

            def group_hi(group, bank, before, c, ends, b):
                kind, i, db = group
                psum = (group_bank + turn_bank)[bank]
                if kind == "L" or not ends:
                    return
                act.wait_ge(psum_ready[kind], nth(group, b))
                if kind in "KQ":
                    need(act, scores_ready, 2 * TB * (PAIRS * (b + db) + i - 1))
                    for e in range(2):
                        rows = slice(HD * e, HD * e + HD)
                        to = KS[rows, i % 2, e, HI] if kind == "K" else QS[rows, i % 2, e]
                        cols = bk_cols if kind == "K" else bq_cols
                        last = nc.scalar.activation(to, psum[rows, :], ACT.Identity, bias=cols[rows, i:i + 1])
                        if e == 0:
                            last.then_inc(hi_ready[kind], 1)
                elif kind == "V":
                    need(act, pv_done, GB * (b + db - 1) + GB // 2 * (i // 2 + 1))
                    j, h = 2 * (i % 2), HEADS // 2 * (i // 2)
                    last = nc.scalar.copy(VS[:, j:j + 2, h:h + 4, HI],
                                          psum[:].rearrange("p (j h d) -> p j h d", j=2, d=HD))
                elif kind == "X":
                    last = nc.scalar.activation(hT[:, HI, i], psum[:], ACT.Relu)
                elif kind == "G":
                    last = nc.scalar.copy(H1[:, HI, i].rearrange("p t n -> p (t n)"), psum[:])
                elif kind == "A":
                    last = nc.scalar.mul(AT[:, HI, i], psum[:], dis[:, i:i + 1])
                last.then_inc(hi_ready[kind], 1)

            def exponent(b, h, i):
                g = GB * b + TB * h + i
                act.wait_ge(masked, g + 1)
                if i == 0:
                    need(act, turned, TB * (HEADS * b + h - 1))
                nc.scalar.activation(probs[:, h % 2, i], score_bank[i % 2][:], ACT.Exp, scale=-1.0,
                                     bias=nmin[:, h, i:i + 1], accum_out=sums[:, h, i:i + 1]).then_inc(exp_done, 1)

            def pt_hi_part(b, h, j):
                k = GB * b + TB * h + j
                act.wait_ge(turned, k + 1)
                need(act, pv_done, k - 3)
                nc.scalar.copy(PT[:, j, HI], turn_bank[j % 2][:]).then_inc(pt_hi, 1)

            def o_lower_half(b, h):
                act.wait_ge(pv_done, GB * b + TB * (h + 1))
                need(act, att_added, PAIRS * b + h // 2)
                rows = slice(HD * (h % 2), HD * (h % 2) + HD)
                nc.scalar.copy(osum[rows].rearrange("p i n -> p (i n)"), o_bank[h % 2][HD:P, :]).then_inc(o_lower, 1)

            def h1_hi_part(b, t):
                act.wait_ge(normed[1], TB * b + t + 1)
                nc.scalar.activation(H1[:, HI, :, t], acc[:, t].rearrange("p (c n) -> p c n", n=P),
                                     ACT.Relu).then_inc(h1_hi, 1)

            def batch(b, first=False, last=False):
                todo = quarters(first, last)
                for h in range(HEADS):
                    for q in range(TB):
                        if q == 2:
                            if h > 0:
                                o_lower_half(b, h - 1)
                            elif not first:
                                o_lower_half(b - 1, HEADS - 1)
                        if q > 0:
                            pt_hi_part(b, h, q - 1)
                        elif h > 0:
                            pt_hi_part(b, h - 1, TB - 1)
                        elif not first:
                            pt_hi_part(b - 1, HEADS - 1, TB - 1)
                        for part in soon(todo, h, q):
                            group_hi(*part, b)
                        for t in range(TB):
                            if not first and X1_HI[t] == (h, q):
                                h1_hi_part(b - 1, t)
                        if h + 1 < HEADS:
                            exponent(b, h + 1, q)
                        elif not last:
                            exponent(b + 1, 0, q)
                        for part in late(todo, h, q):
                            group_hi(*part, b)

            before = straight(BEFORE)
            split_hi(WK, probs[:, 0], wk_loaded)
            for part in before[:CB]:
                group_hi(*part, 0)
            split_hi(WQ, probs[:, 1], wq_loaded, -SCALE)
            act.wait_ge(adj_loaded, 16)
            for t in range(TB):
                nc.scalar.activation(mask[:, t], mask[:, t], ACT.Copy, accum_out=deg[:, t:t + 1]).then_inc(deg_step, 1)
            act.wait_ge(cols_loaded, 32)
            act.wait_ge(bq_scaled, 1)
            for part in before[CB:CB + 8]:
                group_hi(*part, 0)
            split_hi(WV, acc[:], wv_loaded)
            act.wait_ge(w_split, 2)
            exponent(0, 0, 0)
            exponent(0, 0, 1)
            act.wait_ge(dis_ready, 1)
            for part in before[CB + 8:-4]:
                group_hi(*part, 0)
            exponent(0, 0, 2)
            exponent(0, 0, 3)
            for part in before[-4:]:
                group_hi(*part, 0)
            split_hi(W1, res[:], w1_loaded)
            batch(0, first=True)
            with act.Fori(1, BATCH - 1) as b:
                batch(b)
            batch(BATCH - 1, last=True)
            pt_hi_part(BATCH - 1, HEADS - 1, TB - 1)
            o_lower_half(BATCH - 1, HEADS - 1)
            for t in range(TB):
                h1_hi_part(BATCH - 1, t)
            for part in straight(AFTER, ((0, ("L", 2, -2)), (1, ("L", 3, -2)))):
                group_hi(*part, BATCH)

        @block.vector
        def _(dve):
            def split_lo(w, raw, count, scale=1.0):
                dve.wait_ge(w_hi, count)
                nc.vector.scalar_tensor_tensor(w[:, LO], raw, scale, w[:, HI].bitcast(F32), ALU.mult,
                                               ALU.subtract).then_inc(w_split, 1)

            def group_lo(group, bank, before, c, ends, b):
                kind, i, db = group
                psum = (group_bank + turn_bank)[bank]
                if not ends:
                    return
                if kind == "L":
                    dve.wait_ge(psum_ready["L"], nth(group, b))
                    last = nc.vector.tensor_tensor(res[:, i], psum[:], res[:, i], ALU.add)
                elif kind not in "KQ":
                    dve.wait_ge(hi_ready[kind], nth(group, b))
                if kind in "KQ":
                    for e in range(2):
                        dve.wait_ge(hi_ready[kind], 2 * nth(group, b) - 1 + e)
                        rows, other = slice(HD * e, HD * e + HD), slice(HD * (1 - e), HD * (1 - e) + HD)
                        hi = KS[rows, i % 2, e, HI] if kind == "K" else QS[rows, i % 2, e]
                        lo = KS[rows, i % 2, e, LO] if kind == "K" else QS[other, i % 2, e]
                        cols = bk_cols if kind == "K" else bq_cols
                        last = nc.vector.scalar_tensor_tensor(lo, psum[rows, :], cols[rows, i:i + 1],
                                                              hi.bitcast(F32), ALU.add, ALU.subtract)
                elif kind == "V":
                    j, h = 2 * (i % 2), HEADS // 2 * (i // 2)
                    last = nc.vector.tensor_tensor(VS[:, j:j + 2, h:h + 4, LO],
                                                   psum[:].rearrange("p (j h d) -> p j h d", j=2, d=HD),
                                                   VS[:, j:j + 2, h:h + 4, HI].bitcast(F32), ALU.subtract)
                elif kind == "X":
                    last = nc.vector.scalar_tensor_tensor(hT[:, LO, i], psum[:], 0.0, hT[:, HI, i].bitcast(F32),
                                                          ALU.max, ALU.subtract)
                elif kind == "G":
                    last = nc.vector.tensor_tensor(H1[:, LO, i].rearrange("p t n -> p (t n)"), psum[:],
                                                   H1[:, HI, i].rearrange("p t n -> p (t n)").bitcast(F32),
                                                   ALU.subtract)
                elif kind == "A":
                    last = nc.vector.scalar_tensor_tensor(AT[:, LO, i], psum[:], dis[:, i:i + 1],
                                                          AT[:, HI, i].bitcast(F32), ALU.mult, ALU.subtract)
                last.then_inc(done[kind], 1)

            def mask_scores(b, h, i):
                dve.wait_ge(scores_ready, GB * b + TB * h + i + 1)
                nc.vector.sem_inc(dve_gate, 1)
                nc.vector.tensor_tensor_reduce(score_bank[i % 2][:], score_bank[i % 2][:], mask[:, i], 1.0, 3.4e38,
                                               ALU.add, ALU.min, nmin[:, h, i:i + 1]).then_inc(masked, 1)

            def pt_lo_part(b, h, j):
                dve.wait_ge(pt_hi, GB * b + TB * h + j + 1)
                nc.vector.tensor_tensor(PT[:, j, LO], turn_bank[j % 2][:], PT[:, j, HI].bitcast(F32),
                                        ALU.subtract).then_inc(pt_done, 1)

            def o_add(b, h):
                dve.wait_ge(o_lower, HEADS * b + h + 1)
                rows = slice(HD * (h % 2), HD * (h % 2) + HD)
                both = osum[rows].rearrange("p i n -> p (i n)")
                nc.vector.tensor_tensor(both, o_bank[h % 2][0:HD, :], both, ALU.add).then_inc(o_done, 1)

            def invert_sums(b, p):
                dve.wait_ge(exp_done, 2 * TB * (PAIRS * b + p + 1))
                nc.vector.reciprocal(sums[:, 2 * p:2 * p + 2], sums[:, 2 * p:2 * p + 2]).then_inc(rsums_done, 1)

            def normalise_out(b, p):
                dve.wait_ge(rsums_done, PAIRS * b + p + 1)
                dve.wait_ge(o_turned, PAIRS * b + p + 1)
                nc.vector.tensor_tensor(
                    osum[:].rearrange("p i (h d) -> p i h d", d=HD),
                    o_bank[1][:].rearrange("p (i h d) -> p i h d", i=TB, d=HD),
                    sums[:, 2 * p:2 * p + 2].rearrange("p h i -> p i h").unsqueeze(3).to_broadcast([P, TB, 2, HD]),
                    ALU.mult).then_inc(att_done, 1)

            def ln_stats(n, b, src, t):
                nc.vector.bn_stats(ln[n]["stats"][:, t], src[:, t]).then_inc(stats_done[n], 1)

            def ln_moments(n, b):
                for t in range(TB):
                    if t == 0:
                        dve.wait_ge(stats_done[n], TB * (b + 1))
                        nc.vector.sem_inc(dve_gate, 1)
                    nc.vector.bn_aggr(ln[n]["mv"][:, t], ln[n]["stats"][:, t]).then_inc(moments_done[n], 1)
                dve.wait_ge(moments_done[n], TB * (b + 1))
                nc.vector.tensor_scalar(ln[n]["var"][:], ln[n]["mv"][:, :, 1], EPS, None, ALU.add).then_inc(var_done[n], 1)

            def ln_apply(n, b, src, t):
                if t == 0:
                    dve.wait_ge(rstd_done[n], b + 1)
                nc.vector.tensor_scalar(src[:, t], src[:, t], ln[n]["mv"][:, t, 0:1], ln[n]["rstd"][:, t:t + 1],
                                        ALU.subtract, ALU.mult).then_inc(normed[n], 1)

            def h1_lo_part(b, t):
                dve.wait_ge(h1_hi, TB * b + t + 1)
                nc.vector.scalar_tensor_tensor(H1[:, LO, :, t], acc[:, t].rearrange("p (c n) -> p c n", n=P), 0.0,
                                               H1[:, HI, :, t].bitcast(F32), ALU.max, ALU.subtract).then_inc(h1_done, 1)

            def batch(b, first=False, last=False):
                todo = quarters(first, last)
                for h in range(HEADS):
                    for q in range(TB):
                        if h + 1 < HEADS:
                            mask_scores(b, h + 1, q)
                        elif not last:
                            mask_scores(b + 1, 0, q)
                        if q > 0:
                            pt_lo_part(b, h, q - 1)
                        elif h > 0:
                            pt_lo_part(b, h - 1, TB - 1)
                        elif not first:
                            pt_lo_part(b - 1, HEADS - 1, TB - 1)
                        for part in soon(todo, h, q):
                            group_lo(*part, b)
                        if q == 2:
                            if h > 0:
                                o_add(b, h - 1)
                            elif not first:
                                o_add(b - 1, HEADS - 1)
                        if h % 2 == 1 and (h > 1 or not first):
                            bb, p = (b, h // 2 - 1) if h > 1 else (b - 1, PAIRS - 1)
                            if q == 0:
                                invert_sums(bb, p)
                                normalise_out(bb, p)
                        if not first:
                            ln_x1(b - 1, h, q)
                        if not last:
                            ln_x(b + 1, h, q)
                        for part in late(todo, h, q):
                            group_lo(*part, b)

            def ln_x1(b, h, q):
                for t in range(TB):
                    if X1_STATS[t] == (h, q):
                        if t == 0:
                            dve.wait_ge(att_added, PAIRS * (b + 1))
                        ln_stats(1, b, acc, t)
                        if t == TB - 1:
                            ln_moments(1, b)
                    if X1_APPLY[t] == (h, q):
                        if t == 0:
                            dve.wait_ge(res_ready, PAIRS * (b + 1))
                        ln_apply(1, b, acc, t)
                    if X1_LO[t] == (h, q):
                        h1_lo_part(b, t)

            def ln_x(b, h, q):
                for t in range(TB):
                    if X_STATS[t] == (h, q):
                        if t == 0:
                            dve.wait_ge(x_loaded, 16 * b)
                        ln_stats(0, b, hn, t)
                        if t == TB - 1:
                            ln_moments(0, b)
                    if X_APPLY[t] == (h, q):
                        ln_apply(0, b, hn, t)

            nc.vector.memset(half[:], -0.5).then_inc(consts_ready, 1)
            for t in range(TB):
                dve.wait_ge(x0_loaded[t], 16)
                ln_stats(0, 0, hn, t)
            ln_moments(0, 0)
            for t in range(TB):
                ln_apply(0, 0, hn, t)
            before = straight(BEFORE)
            split_lo(WK, probs[:, 0], 1)
            for part in before[:CB]:
                group_lo(*part, 0)
            split_lo(WQ, probs[:, 1], 2, -SCALE)
            dve.wait_ge(cols_loaded, 32)
            nc.vector.tensor_scalar(bq_cols[:], bq_cols[:], -SCALE, None, ALU.mult).then_inc(bq_scaled, 1)
            dve.wait_ge(deg_step, TB)
            nc.vector.tensor_scalar(dpos[:], deg[:], 0.0, None, ALU.is_gt).then_inc(deg_step, 1)
            dve.wait_ge(deg_step, TB + 1)
            nc.vector.tensor_scalar(deg[:], deg[:], 1.1754944e-38, None, ALU.max).then_inc(deg_step, 1)
            for part in before[CB:CB + 4]:
                group_lo(*part, 0)
            dve.wait_ge(deg_pow, 1)
            nc.vector.tensor_tensor(dis[:], dis[:], dpos[:], ALU.mult).then_inc(dis_ready, 1)
            dve.wait_ge(dis_ready, 1)
            dve.wait_ge(psum_ready["X"], CB)
            for t in range(TB):
                last = nc.vector.tensor_scalar(hn[:, t], mask[:, t], dis[:, t:t + 1], None, ALU.mult)
            last.then_inc(adj_scaled, 1)
            dve.wait_ge(adj_scaled, 1)
            nc.vector.tensor_scalar(mask[:], mask[:], 0.0, MASKED, ALU.is_equal, ALU.mult).then_inc(mask_ready, 1)
            for part in before[CB + 4:CB + 8]:
                group_lo(*part, 0)
            split_lo(WV, acc[:], 3)
            dve.wait_ge(mask_ready, 1)
            mask_scores(0, 0, 0)
            mask_scores(0, 0, 1)
            for part in before[CB + 8:-4]:
                group_lo(*part, 0)
            mask_scores(0, 0, 2)
            mask_scores(0, 0, 3)
            for part in before[-4:]:
                group_lo(*part, 0)
            split_lo(W1, res[:], 4)
            batch(0, first=True)
            with dve.Fori(1, BATCH - 1) as b:
                batch(b)
            batch(BATCH - 1, last=True)
            pt_lo_part(BATCH - 1, HEADS - 1, TB - 1)
            o_add(BATCH - 1, HEADS - 1)
            invert_sums(BATCH - 1, PAIRS - 1)
            normalise_out(BATCH - 1, PAIRS - 1)
            dve.wait_ge(att_added, PAIRS * BATCH)
            for t in range(TB):
                ln_stats(1, BATCH - 1, acc, t)
            ln_moments(1, BATCH - 1)
            dve.wait_ge(res_ready, PAIRS * BATCH)
            for t in range(TB):
                ln_apply(1, BATCH - 1, acc, t)
            for t in range(TB):
                h1_lo_part(BATCH - 1, t)
            for part in straight(AFTER, ((0, ("L", 2, -2)), (1, ("L", 3, -2)))):
                group_lo(*part, BATCH)

        @block.gpsimd
        def _(pool):
            def rstd(n, b):
                pool.wait_ge(var_done[n], b + 1)
                nc.gpsimd.tensor_tensor(ln[n]["rstd"][:], ln[n]["var"][:], half[:], ALU.pow).then_inc(rstd_done[n], 1)

            def add_bv(b, p):
                if p == 0:
                    pool.wait_ge(acc_loaded, 16 * TB * (b + 1))
                cols = slice(P * p, P * p + P)
                nc.gpsimd.tensor_tensor(acc[:, :, cols], acc[:, :, cols],
                                        bv_rows[:, cols].unsqueeze(1).to_broadcast([P, TB, P]),
                                        ALU.add).then_inc(acc_biased, 1)

            def add_attention(b, p):
                pool.wait_ge(att_done, PAIRS * b + p + 1)
                pool.wait_ge(acc_biased, PAIRS * b + p + 1)
                cols = slice(P * p, P * p + P)
                nc.gpsimd.tensor_tensor(acc[:, :, cols], acc[:, :, cols], osum[:], ALU.add).then_inc(att_added, 1)

            def add_bias(b, p):
                if p == 0:
                    pool.wait_ge(res_free, 16 + 16 * TB * b)
                pool.wait_ge(att_added, PAIRS * b + p + 1)
                cols = slice(P * p, P * p + P)
                nc.gpsimd.tensor_tensor(res[:, :, cols], acc[:, :, cols],
                                        b1_rows[:, cols].unsqueeze(1).to_broadcast([P, TB, P]),
                                        ALU.add).then_inc(res_ready, 1)

            def batch(b, first=False, last=False):
                if not last:
                    rstd(0, b + 1)
                if not first:
                    add_attention(b - 1, PAIRS - 1)
                    add_bias(b - 1, PAIRS - 1)
                    rstd(1, b - 1)
                add_bv(b, 0)
                add_attention(b, 0)
                add_bv(b, 1)
                add_attention(b, 1)
                add_bv(b, 2)
                add_attention(b, 2)
                add_bv(b, 3)
                for p in range(PAIRS - 1):
                    add_bias(b, p)

            nc.gpsimd.memset(ident[:], 0.0).then_inc(consts_ready, 1)
            pool.wait_ge(consts_ready, 2)
            nc.gpsimd.affine_select(out=ident[:], in_=ident[:], compare_op=ALU.not_equal, fill=1.0, base=0,
                                    pattern=[[-1, P]], channel_multiplier=1).then_inc(ident_ready, 1)
            rstd(0, 0)
            pool.wait_ge(deg_step, TB + 2)
            nc.gpsimd.tensor_tensor(dis[:], deg[:], half[:], ALU.pow).then_inc(deg_pow, 1)
            pool.wait_ge(rows_loaded, 16)
            batch(0, first=True)
            with pool.Fori(1, BATCH - 1) as b:
                batch(b)
            batch(BATCH - 1, last=True)
            add_attention(BATCH - 1, PAIRS - 1)
            add_bias(BATCH - 1, PAIRS - 1)
            rstd(1, BATCH - 1)


_INS = ['x', 'adj', 'L0_gnn_Wq', 'L0_gnn_bq', 'L0_gnn_Wk', 'L0_gnn_bk', 'L0_gnn_Wv', 'L0_gnn_bv',
        'L1_gnn_weight', 'L1_gnn_bias']


def kernel(**inputs):
    import numpy as _np
    import concourse.bacc as _bacc
    from concourse import mybir as _mybir
    from concourse.bass_utils import run_bass_kernel_spmd as _run

    nc = _bacc.Bacc("TRN2", target_bir_lowering=False, num_devices=1, dynamic_dma_scratch_size=512)
    arrays, args = {}, []
    for name in _INS:
        a = _np.ascontiguousarray(inputs[name])
        arrays[f"in_{name}_dram"] = a
        args.append(nc.dram_tensor(f"in_{name}_dram", a.shape, _mybir.dt.from_np(a.dtype), kind="ExternalInput").ap())
    out = nc.dram_tensor("out_dram", (BATCH, TOK, DIM), _mybir.dt.float32, kind="ExternalOutput").ap()
    gnn_layers(nc, *args, out)
    r = _run(nc, [arrays], core_ids=[0])
    return r.results[0]["out_dram"]
```
